# Optimizing a Trainium2 kernel written in Bass

```python
import numpy as np
import jax
import jax.numpy as jnp

def _softmax(x, axis=-1):
    return jax.nn.softmax(x, axis=axis)

def _gelu(x):
    return jax.nn.gelu(x, approximate=True)

def _silu(x):
    return jax.nn.silu(x)

def _sigmoid(x):
    return jax.nn.sigmoid(x)

def _layernorm(x, axis=-1, eps=1e-05):
    m = jnp.mean(x, axis=axis, keepdims=True)
    v = jnp.var(x, axis=axis, keepdims=True)
    return (x - m) / jnp.sqrt(v + eps)

def _scatter_add(tgt, idx, src, axis=0):
    return tgt.at[idx].add(src)

def _segment_sum(src, seg, n):
    return jax.ops.segment_sum(src, seg, n)
kernel_name = 'mk_xattn_seq_d2_seqx_r4_c74881'

def setup_inputs(seed: int=0):
    np.random.seed(seed)
    _w = jnp.asarray

    def _rec_inputs():
        import jax
        import jax.numpy as jnp
        _rk = jax.random.key(seed)
        x = 7.22e-05 + 1 * jax.random.normal(jax.random.fold_in(_rk, 1), (16, 256, 256), jnp.float32)
        _lenS = 256 - jax.random.randint(jax.random.fold_in(_rk, 7), (16,), 0, max(1, 256 // 4) + 1, jnp.int32)
        _lenS2 = 256 - jax.random.randint(jax.random.fold_in(_rk, 8), (16,), 0, max(1, 256 // 4) + 1, jnp.int32)
        _ctx_1024P = jax.random.normal(jax.random.fold_in(_rk, 11), (16, 16, 256), jnp.float32)
        _ctx_1024c = jax.random.dirichlet(jax.random.fold_in(_rk, 511), 0.3 * jnp.ones((16,), jnp.float32), (16, 256))
        _ctx_1024t = jnp.einsum('bsk,bkd->bsd', _ctx_1024c, _ctx_1024P)
        _ctx_1024t = _ctx_1024t * jax.lax.rsqrt(jnp.mean(jnp.square(_ctx_1024t)) + 1e-12) * 0.953939
        ctx_1024 = 4.13588e-05 + 0.999923 * (_ctx_1024t + 0.3 * jax.random.normal(jax.random.fold_in(_rk, 611), (16, 256, 256), jnp.float32))
        _validS = jnp.arange(256)[None, :] < _lenS[:, None]
        _validS2 = jnp.arange(256)[None, :] < _lenS2[:, None]
        _causal = jnp.tril(jnp.ones((256, 256), dtype=bool))
        mask_BxSxS2_fk0 = jnp.where(jnp.broadcast_to(_validS2[:, None, :], (16, 256, 256)), 0.0, 1.0).astype(jnp.float32)
        return (x, ctx_1024, mask_BxSxS2_fk0)
    x, ctx_1024, mask_BxSxS2_fk0 = _rec_inputs()

    def _L0_xattn_setup():
        import jax, jax.numpy as jnp
        import numpy as np
        import math
        B, S, D, H, FF = (4, 512, 256, 16, 1024)
        HD = D // H
        EPS = 1e-05

        def _layer_norm(x, g, b):
            m = jnp.mean(x, axis=-1, keepdims=True)
            v = jnp.mean((x - m) ** 2, axis=-1, keepdims=True)
            return (x - m) * jax.lax.rsqrt(v + EPS) * g + b

        def _self_attn(x, mask, Wq, bq, Wk, bk, Wv, bv, Wo, bo):
            b, s, d = x.shape
            q = (x @ Wq.T + bq).reshape(b, s, H, HD)
            k = (x @ Wk.T + bk).reshape(b, s, H, HD)
            v = (x @ Wv.T + bv).reshape(b, s, H, HD)
            score = jnp.einsum('bshd,bthd->bhst', q, k) / math.sqrt(HD)
            score = score + (1.0 - mask[:, None, :, :]) * -1000000000.0
            p = jax.nn.softmax(score, axis=-1)
            o = jnp.einsum('bhst,bthd->bshd', p, v).reshape(b, s, d)
            return o @ Wo.T + bo
        key = jax.random.key(seed)
        ks = jax.random.split(key, 16)
        sd = 0.02
        inp = {'tgt': jax.random.normal(ks[0], (B, S, D), jnp.float32), 'memory': jax.random.normal(ks[1], (B, S, D), jnp.float32), 'mask': jnp.broadcast_to(jnp.tril(jnp.ones((S, S), jnp.float32)), (B, S, S)), 'Wq': jax.random.normal(ks[2], (D, D), jnp.float32) * sd, 'bq': jnp.zeros((D,), jnp.float32), 'Wk': jax.random.normal(ks[3], (D, D), jnp.float32) * sd, 'bk': jnp.zeros((D,), jnp.float32), 'Wv': jax.random.normal(ks[4], (D, D), jnp.float32) * sd, 'bv': jnp.zeros((D,), jnp.float32), 'Wo': jax.random.normal(ks[5], (D, D), jnp.float32) * sd, 'bo': jnp.zeros((D,), jnp.float32), 'Wg': jax.random.normal(ks[6], (D, D), jnp.float32) * sd, 'bg': jnp.zeros((D,), jnp.float32), 'W1': jax.random.normal(ks[7], (FF, D), jnp.float32) * sd, 'b1': jnp.zeros((FF,), jnp.float32), 'W2': jax.random.normal(ks[8], (D, FF), jnp.float32) * sd, 'b2': jnp.zeros((D,), jnp.float32), 'g1': jnp.ones((D,), jnp.float32), 'be1': jnp.zeros((D,), jnp.float32), 'g2': jnp.ones((D,), jnp.float32), 'be2': jnp.zeros((D,), jnp.float32)}
        return inp
    _L0_xattn_all = _L0_xattn_setup()
    _L0_xattn_in = {k: v for k, v in _L0_xattn_all.items() if k in ('Wq', 'bq', 'Wk', 'bk', 'Wv', 'bv', 'Wo', 'bo', 'Wg', 'bg', 'W1', 'b1', 'W2', 'b2', 'g1', 'be1', 'g2', 'be2')}
    del _L0_xattn_all

    def _L1_xattn_setup():
        import jax, jax.numpy as jnp
        import numpy as np
        NUM_HEADS = 16
        EPS = 1e-06
        NEG_INF = -1000000000.0

        def layer_norm(x, scale, bias):
            m = jnp.mean(x, axis=-1, keepdims=True)
            v = jnp.mean(jnp.square(x - m), axis=-1, keepdims=True)
            return (x - m) * jax.lax.rsqrt(v + EPS) * scale + bias

        def mha(x_q, x_kv, wq, wk, wv, wo, causal):
            B, Sq, D = x_q.shape
            Sk = x_kv.shape[1]
            H = NUM_HEADS
            Dh = D // H
            q = (x_q @ wq).reshape(B, Sq, H, Dh) * (1.0 / np.sqrt(Dh))
            k = (x_kv @ wk).reshape(B, Sk, H, Dh)
            v = (x_kv @ wv).reshape(B, Sk, H, Dh)
            scores = jnp.einsum('bqhf,bkhf->bhqk', q, k)
            if causal:
                mask = jnp.tril(jnp.ones((Sq, Sk), dtype=bool))
                scores = jnp.where(mask, scores, NEG_INF)
            p = jax.nn.softmax(scores, axis=-1)
            o = jnp.einsum('bhqk,bkhf->bqhf', p, v).reshape(B, Sq, D)
            return o @ wo
        key = jax.random.key(seed)
        ks = jax.random.split(key, 12)
        B, S, D, F = (2, 512, 256, 1024)
        w = 0.02
        return {'targets': jax.random.normal(ks[0], (B, S, D), jnp.float32), 'encoded': jax.random.normal(ks[1], (B, S, D), jnp.float32), 'ln1_s': jnp.ones((D,), jnp.float32), 'ln1_b': jnp.zeros((D,), jnp.float32), 'sa_wq': jax.random.normal(ks[2], (D, D), jnp.float32) * w, 'sa_wk': jax.random.normal(ks[3], (D, D), jnp.float32) * w, 'sa_wv': jax.random.normal(ks[4], (D, D), jnp.float32) * w, 'sa_wo': jax.random.normal(ks[5], (D, D), jnp.float32) * w, 'ln2_s': jnp.ones((D,), jnp.float32), 'ln2_b': jnp.zeros((D,), jnp.float32), 'ca_wq': jax.random.normal(ks[6], (D, D), jnp.float32) * w, 'ca_wk': jax.random.normal(ks[7], (D, D), jnp.float32) * w, 'ca_wv': jax.random.normal(ks[8], (D, D), jnp.float32) * w, 'ca_wo': jax.random.normal(ks[9], (D, D), jnp.float32) * w, 'ln3_s': jnp.ones((D,), jnp.float32), 'ln3_b': jnp.zeros((D,), jnp.float32), 'mlp_w1': jax.random.normal(ks[10], (D, F), jnp.float32) * w, 'mlp_b1': jnp.zeros((F,), jnp.float32), 'mlp_w2': jax.random.normal(ks[11], (F, D), jnp.float32) * w, 'mlp_b2': jnp.zeros((D,), jnp.float32)}
    _L1_xattn_all = _L1_xattn_setup()
    _L1_xattn_in = {k: v for k, v in _L1_xattn_all.items() if k in ('ln1_s', 'ln1_b', 'sa_wq', 'sa_wk', 'sa_wv', 'sa_wo', 'ln2_s', 'ln2_b', 'ca_wq', 'ca_wk', 'ca_wv', 'ca_wo', 'ln3_s', 'ln3_b', 'mlp_w1', 'mlp_b1', 'mlp_w2', 'mlp_b2')}
    del _L1_xattn_all
    return {'x': x, 'ctx_1024': ctx_1024, 'mask_BxSxS2_fk0': mask_BxSxS2_fk0, 'L0_xattn_Wq': _L0_xattn_in['Wq'], 'L0_xattn_bq': _L0_xattn_in['bq'], 'L0_xattn_Wk': _L0_xattn_in['Wk'], 'L0_xattn_bk': _L0_xattn_in['bk'], 'L0_xattn_Wv': _L0_xattn_in['Wv'], 'L0_xattn_bv': _L0_xattn_in['bv'], 'L0_xattn_Wo': _L0_xattn_in['Wo'], 'L0_xattn_bo': _L0_xattn_in['bo'], 'L0_xattn_Wg': _L0_xattn_in['Wg'], 'L0_xattn_bg': _L0_xattn_in['bg'], 'L0_xattn_W1': _L0_xattn_in['W1'], 'L0_xattn_b1': _L0_xattn_in['b1'], 'L0_xattn_W2': _L0_xattn_in['W2'], 'L0_xattn_b2': _L0_xattn_in['b2'], 'L0_xattn_g1': _L0_xattn_in['g1'], 'L0_xattn_be1': _L0_xattn_in['be1'], 'L0_xattn_g2': _L0_xattn_in['g2'], 'L0_xattn_be2': _L0_xattn_in['be2'], 'L1_xattn_ln1_s': _L1_xattn_in['ln1_s'], 'L1_xattn_ln1_b': _L1_xattn_in['ln1_b'], 'L1_xattn_sa_wq': _L1_xattn_in['sa_wq'], 'L1_xattn_sa_wk': _L1_xattn_in['sa_wk'], 'L1_xattn_sa_wv': _L1_xattn_in['sa_wv'], 'L1_xattn_sa_wo': _L1_xattn_in['sa_wo'], 'L1_xattn_ln2_s': _L1_xattn_in['ln2_s'], 'L1_xattn_ln2_b': _L1_xattn_in['ln2_b'], 'L1_xattn_ca_wq': _L1_xattn_in['ca_wq'], 'L1_xattn_ca_wk': _L1_xattn_in['ca_wk'], 'L1_xattn_ca_wv': _L1_xattn_in['ca_wv'], 'L1_xattn_ca_wo': _L1_xattn_in['ca_wo'], 'L1_xattn_ln3_s': _L1_xattn_in['ln3_s'], 'L1_xattn_ln3_b': _L1_xattn_in['ln3_b'], 'L1_xattn_mlp_w1': _L1_xattn_in['mlp_w1'], 'L1_xattn_mlp_b1': _L1_xattn_in['mlp_b1'], 'L1_xattn_mlp_w2': _L1_xattn_in['mlp_w2'], 'L1_xattn_mlp_b2': _L1_xattn_in['mlp_b2']}

def reference(x, ctx_1024, mask_BxSxS2_fk0, L0_xattn_Wq, L0_xattn_bq, L0_xattn_Wk, L0_xattn_bk, L0_xattn_Wv, L0_xattn_bv, L0_xattn_Wo, L0_xattn_bo, L0_xattn_Wg, L0_xattn_bg, L0_xattn_W1, L0_xattn_b1, L0_xattn_W2, L0_xattn_b2, L0_xattn_g1, L0_xattn_be1, L0_xattn_g2, L0_xattn_be2, L1_xattn_ln1_s, L1_xattn_ln1_b, L1_xattn_sa_wq, L1_xattn_sa_wk, L1_xattn_sa_wv, L1_xattn_sa_wo, L1_xattn_ln2_s, L1_xattn_ln2_b, L1_xattn_ca_wq, L1_xattn_ca_wk, L1_xattn_ca_wv, L1_xattn_ca_wo, L1_xattn_ln3_s, L1_xattn_ln3_b, L1_xattn_mlp_w1, L1_xattn_mlp_b1, L1_xattn_mlp_w2, L1_xattn_mlp_b2):
    import jax
    import jax.numpy as jnp

    def _L0_xattn_ref(tgt, memory, mask, Wq, bq, Wk, bk, Wv, bv, Wo, bo, Wg, bg, W1, b1, W2, b2, g1, be1, g2, be2):
        import jax, jax.numpy as jnp
        import numpy as np
        import math
        B, S, D, H, FF = (4, 512, 256, 16, 1024)
        HD = D // H
        EPS = 1e-05

        def _layer_norm(x, g, b):
            m = jnp.mean(x, axis=-1, keepdims=True)
            v = jnp.mean((x - m) ** 2, axis=-1, keepdims=True)
            return (x - m) * jax.lax.rsqrt(v + EPS) * g + b

        def _self_attn(x, mask, Wq, bq, Wk, bk, Wv, bv, Wo, bo):
            b, s, d = x.shape
            q = (x @ Wq.T + bq).reshape(b, s, H, HD)
            k = (x @ Wk.T + bk).reshape(b, s, H, HD)
            v = (x @ Wv.T + bv).reshape(b, s, H, HD)
            score = jnp.einsum('bshd,bthd->bhst', q, k) / math.sqrt(HD)
            score = score + (1.0 - mask[:, None, :, :]) * -1000000000.0
            p = jax.nn.softmax(score, axis=-1)
            o = jnp.einsum('bhst,bthd->bshd', p, v).reshape(b, s, d)
            return o @ Wo.T + bo
        tgt1 = _layer_norm(tgt, g1, be1)
        tgt = tgt + _self_attn(tgt1, mask, Wq, bq, Wk, bk, Wv, bv, Wo, bo)
        tgt = tgt + (memory @ Wg.T + bg)
        tgt1 = _layer_norm(tgt, g2, be2)
        ff = jax.nn.relu(tgt1 @ W1.T + b1) @ W2.T + b2
        return tgt + ff

    def _L1_xattn_ref(targets, encoded, ln1_s, ln1_b, sa_wq, sa_wk, sa_wv, sa_wo, ln2_s, ln2_b, ca_wq, ca_wk, ca_wv, ca_wo, ln3_s, ln3_b, mlp_w1, mlp_b1, mlp_w2, mlp_b2):
        import jax, jax.numpy as jnp
        import numpy as np
        NUM_HEADS = 16
        EPS = 1e-06
        NEG_INF = -1000000000.0

        def layer_norm(x, scale, bias):
            m = jnp.mean(x, axis=-1, keepdims=True)
            v = jnp.mean(jnp.square(x - m), axis=-1, keepdims=True)
            return (x - m) * jax.lax.rsqrt(v + EPS) * scale + bias

        def mha(x_q, x_kv, wq, wk, wv, wo, causal):
            B, Sq, D = x_q.shape
            Sk = x_kv.shape[1]
            H = NUM_HEADS
            Dh = D // H
            q = (x_q @ wq).reshape(B, Sq, H, Dh) * (1.0 / np.sqrt(Dh))
            k = (x_kv @ wk).reshape(B, Sk, H, Dh)
            v = (x_kv @ wv).reshape(B, Sk, H, Dh)
            scores = jnp.einsum('bqhf,bkhf->bhqk', q, k)
            if causal:
                mask = jnp.tril(jnp.ones((Sq, Sk), dtype=bool))
                scores = jnp.where(mask, scores, NEG_INF)
            p = jax.nn.softmax(scores, axis=-1)
            o = jnp.einsum('bhqk,bkhf->bqhf', p, v).reshape(B, Sq, D)
            return o @ wo
        x = layer_norm(targets, ln1_s, ln1_b)
        x = mha(x, x, sa_wq, sa_wk, sa_wv, sa_wo, causal=True)
        x = x + targets
        y = layer_norm(x, ln2_s, ln2_b)
        y = mha(y, encoded, ca_wq, ca_wk, ca_wv, ca_wo, causal=False)
        y = y + x
        z = layer_norm(y, ln3_s, ln3_b)
        z = jax.nn.relu(z @ mlp_w1 + mlp_b1) @ mlp_w2 + mlp_b2
        return y + z
    x = _L0_xattn_ref(x, ctx_1024, mask_BxSxS2_fk0, L0_xattn_Wq, L0_xattn_bq, L0_xattn_Wk, L0_xattn_bk, L0_xattn_Wv, L0_xattn_bv, L0_xattn_Wo, L0_xattn_bo, L0_xattn_Wg, L0_xattn_bg, L0_xattn_W1, L0_xattn_b1, L0_xattn_W2, L0_xattn_b2, L0_xattn_g1, L0_xattn_be1, L0_xattn_g2, L0_xattn_be2)
    x = _L1_xattn_ref(x, ctx_1024, L1_xattn_ln1_s, L1_xattn_ln1_b, L1_xattn_sa_wq, L1_xattn_sa_wk, L1_xattn_sa_wv, L1_xattn_sa_wo, L1_xattn_ln2_s, L1_xattn_ln2_b, L1_xattn_ca_wq, L1_xattn_ca_wk, L1_xattn_ca_wv, L1_xattn_ca_wo, L1_xattn_ln3_s, L1_xattn_ln3_b, L1_xattn_mlp_w1, L1_xattn_mlp_b1, L1_xattn_mlp_w2, L1_xattn_mlp_b2)
    return x

_drawn_inputs = setup_inputs


def setup_inputs(seed=0):
    import zlib

    import numpy as np

    out = dict(_drawn_inputs(seed))
    spreads = {'L0_xattn_bq': (0.0, 0.8),
     'L0_xattn_bk': (0.0, 0.8),
     'L0_xattn_bv': (0.0, 0.1),
     'L0_xattn_bo': (0.0, 0.1),
     'L0_xattn_bg': (0.0, 0.1),
     'L0_xattn_b1': (0.0, 0.1),
     'L0_xattn_b2': (0.0, 0.1),
     'L0_xattn_g1': (1.0, 0.6),
     'L0_xattn_be1': (0.0, 0.8),
     'L0_xattn_g2': (1.0, 0.6),
     'L0_xattn_be2': (0.0, 0.593),
     'L1_xattn_ln1_s': (1.0, 0.6),
     'L1_xattn_ln1_b': (0.0, 0.8),
     'L1_xattn_ln2_s': (1.0, 0.6),
     'L1_xattn_ln2_b': (0.0, 0.8),
     'L1_xattn_ln3_s': (1.0, 0.6),
     'L1_xattn_ln3_b': (0.0, 0.604),
     'L1_xattn_mlp_b1': (0.0, 0.1),
     'L1_xattn_mlp_b2': (0.0, 0.1)}
    factors = {'L0_xattn_Wq': 8.0,
     'L0_xattn_Wk': 8.0,
     'L1_xattn_sa_wq': 8.0,
     'L1_xattn_sa_wk': 8.0,
     'L1_xattn_ca_wq': 8.0,
     'L1_xattn_ca_wk': 8.0}
    for name, (base, spread) in spreads.items():
        noise = np.random.default_rng([zlib.crc32(name.encode()), seed]).standard_normal(out[name].shape)
        drawn = base * np.exp(spread * noise) if base else spread * noise
        out[name] = jnp.asarray(drawn.astype(out[name].dtype))
    for name, factor in factors.items():
        out[name] = (out[name] * factor).astype(out[name].dtype)
    return out
```

```python
from contextlib import ExitStack

import concourse.bass as bass
from concourse import mybir

F32 = mybir.dt.float32
F32R = mybir.dt.float32r
BF16 = mybir.dt.bfloat16
ALU = mybir.AluOpType
ACT = mybir.ActivationFunctionType
AX_X = mybir.AxisListType.X

P = 128
B, S, D = 16, 256, 256
H, HD = 16, 16
FF = 1024
KC = D // P
TT = S // P
FT = FF // P
CH = 4
NPASS = 3
MLP = (0, 2)
ALL = (0, 1, 2)
NTASK = NPASS * B
Q_PARTS = (0, 0, 1, 1, 0, 2)
K_PARTS = (0, 1, 0, 1, 2, 0)
NBLK = len(Q_PARTS)
ROWS = NBLK * HD
VW = HD + 1
LN_EPS = (1e-5, 1e-6, 1e-6)
MASKED = 1e9
HUGE = 3e38
WQ, WK, WV, WO, WG = range(5)
C_LN, C_LN2, C_BQ, C_BK, C_B1, NCOL = 0, 12, 20, 22, 24, 40
R_BV, R_BO, R_BG, R_B2, NROW = 0, 1, 2, 3, 5
UNITS = (("a", 0, (WQ, WK, WV)), ("a", 0, (WO, WG)), ("w1", 0, ()), ("w2", 0, ()),
         ("a", 1, (WQ, WK, WV)), ("a", 1, (WO,)), ("w1", 1, ()), ("w2", 1, ()),
         ("a", 2, (WQ, WK, WV)), ("a", 2, (WO,)))
UNIT_AT = {(-2, 14): (0,), (-1, 13): (1,), (0, 3): (2,), (0, 12): (3,),
           (14, 9): (4,), (16, 13): (5,), (17, 9): (6,), (17, 14): (7,), (30, 9): (8,), (32, 13): (9,)}
UNIT_QKV, UNIT_O = {0: 0, 1: 4, 2: 8}, {0: 1, 1: 5, 2: 9}
UNIT_W1, UNIT_W2 = {0: 2, 2: 6}, {0: 3, 2: 7}


class Task:

    def __init__(self, p, c, i=None):
        self.p, self.c, self.i, self.par = p, c, i, c % 2
        self.b = c if i is None else i * 2 + c
        self.first = i is None and c == 0


class Step:

    def __init__(self, s=None, p=0, j=0, i=None):
        self.s = s

        def at(off):
            if i is not None:
                return Task(p, 2 + j + off, i)
            return Task((s + off) // B, (s + off) % B) if 0 <= s + off < NTASK else None

        self.nxt2, self.nxt, self.cur = at(2), at(1), at(0)
        self.prev, self.old, self.older = at(-1), at(-2), at(-3)


def steps(eng, body):
    for s in range(-2, 2):
        body(Step(s))
    for p in range(NPASS):
        with eng.Fori(0, (B - 4) // 2) as i:
            for j in range(2):
                body(Step(p=p, j=j, i=i))
        for s in range(B * p + B - 2, B * p + B + 2):
            body(Step(s))


class Event:

    def __init__(self, sem, per=1, passes=ALL, credit=0):
        self.sem, self.per, self.passes, self.credit = sem, per, passes, credit

    def after(self, task, k=None):
        before = B * sum(q < task.p for q in self.passes)
        if task.p not in self.passes:
            return before * self.per + self.credit
        k = self.per if k is None else k
        const = (before + task.c) * self.per + k + self.credit
        return const if task.i is None else task.i * (2 * self.per) + const


class DmaEvent:

    def __init__(self, sems, dmas=1, passes=ALL, credit=0):
        self.sems, self.dmas, self.passes, self.credit = sems, dmas, passes, credit

    def of(self, task):
        return self.sems[task.par]

    def after(self, task):
        before = B * sum(q < task.p for q in self.passes)
        const = 16 * (self.dmas * ((before + task.c) // 2 + 1) + self.credit)
        return const if task.i is None else task.i * (16 * self.dmas) + const


def two_layers(nc, x, ctx, mask, wa, wm1, wm2, cols, rows, ident, out):
    with ExitStack() as es:
        def sb(name, shape, dt=F32):
            return es.enter_context(nc.sbuf_tensor(name, shape, dt))

        def sem(name):
            return es.enter_context(nc.semaphore(name))

        def ev(name, per=1, passes=ALL, credit=0):
            return Event(sem(name), per, passes, credit)

        def dev(name, dmas=1, passes=ALL, credit=0):
            return DmaEvent([sem(f"{name}_{i}") for i in range(2)], dmas, passes, credit)

        w_hi, w_lo = sb("w_hi", [P, 5, KC, D], F32R), sb("w_lo", [P, 5, KC, D], F32R)
        w1_hi, w1_lo = sb("w1_hi", [P, KC, FF], F32R), sb("w1_lo", [P, KC, FF], F32R)
        w2_hi, w2_lo = sb("w2_hi", [P, FT, D], F32R), sb("w2_lo", [P, FT, D], F32R)
        stage = sb("stage", [P, KC * FF])
        ident_sb = sb("ident_sb", [P, P])
        cols_sb = sb("cols_sb", [P, NCOL])
        rows_sb = sb("rows_sb", [P, NROW, D])
        minus_half = sb("minus_half", [P, TT])
        x_in = sb("x_in", [P, 2, TT, D])
        stats, mv, rstd = sb("stats", [P, TT, 6]), sb("mv", [P, TT, 2]), sb("rstd", [P, TT])
        stats2, mv2, rstd2 = sb("stats2", [P, TT, 6]), sb("mv2", [P, TT, 2]), sb("rstd2", [P, TT])
        ve, ve2 = sb("ve", [P, TT]), sb("ve2", [P, TT])
        tf_a, tf_b = sb("tf_a", [P, KC, S]), sb("tf_b", [P, KC, S])
        xt_hi, xt_lo = sb("xt_hi", [P, KC, S], F32R), sb("xt_lo", [P, KC, S], F32R)
        c_in = sb("c_in", [P, TT, D])
        ct_hi, ct_lo = sb("ct_hi", [P, KC, S], F32R), sb("ct_lo", [P, KC, S], F32R)
        q_f, k_f = sb("q_f", [P, KC, S]), sb("k_f", [P, KC, S])
        q_part, k_part = sb("q_part", [P, 3, KC, S], BF16), sb("k_part", [P, 3, KC, S], BF16)
        q_stack, k_stack = sb("q_stack", [ROWS, 2, H, S], BF16), sb("k_stack", [ROWS, 2, H, S], BF16)
        v_sb = sb("v_sb", [P, 2, TT, H, VW])
        prob = sb("prob", [P, 4, TT, S])
        neg_max = sb("neg_max", [P, 4, TT])
        prob_t = sb("prob_t", [P, 8, TT * S])
        o_t = sb("o_t", [P, CH, S])
        rden = sb("rden", [P, TT, H])
        o_sb = sb("o_sb", [P, TT, D])
        ot_hi, ot_lo = sb("ot_hi", [P, KC, S], F32R), sb("ot_lo", [P, KC, S], F32R)
        x_res = sb("x_res", [P, TT, D])
        x2 = sb("x2", [P, 2, TT, D])
        x2_hat = sb("x2_hat", [P, TT, D])
        x2t_hi, x2t_lo = sb("x2t_hi", [P, KC, S], F32R), sb("x2t_lo", [P, KC, S], F32R)
        h_f = sb("h_f", [P, 2, 2, S])
        h_hi, h_lo = sb("h_hi", [P, FT, S], F32R), sb("h_lo", [P, FT, S], F32R)
        y_sb = sb("y_sb", [P, TT, D])
        bias_sb = sb("bias_sb", [P, 2, TT, S])
        causal = sb("causal", [P, TT, S])

        s_ps = es.enter_context(nc.psum_tensor("s_ps", [P, 2, 512], F32))
        t_ps = es.enter_context(nc.psum_tensor("t_ps", [P, 2, 512], F32))
        o_ps = es.enter_context(nc.psum_tensor("o_ps", [P, 512], F32))
        m_ps = es.enter_context(nc.psum_tensor("m_ps", [P, 512], F32))
        d_ps = es.enter_context(nc.psum_tensor("d_ps", [P, 2, 512], F32))

        x_mid = nc.dram_tensor("x_mid", (2, B, S, D), F32, kind="Internal").ap()
        parts = nc.dram_tensor("parts", (2, 2, 3, H, HD, S), BF16, kind="Internal").ap()

        def tokens(dram):
            return dram.rearrange("(t p) d -> p t d", p=P)

        passed = sem("passed")
        const_landed, unit_landed = sem("const_landed"), sem("unit_landed")
        x_landed, res_landed = dev("x_landed"), dev("res_landed")
        ctx_landed, mask_landed = dev("ctx_landed", 1, MLP), dev("mask_landed", 1, (0,))
        q_written, k_written = dev("q_written", KC), dev("k_written", KC)
        stacked, stored = dev("stacked", 2 * NBLK), dev("stored", credit=1)
        xt_mm, ct_mm, x2t_mm = ev("xt_mm"), ev("ct_mm", 1, MLP), ev("x2t_mm", 1, MLP)
        q_mm, k_mm, v_mm = ev("q_mm"), ev("k_mm"), ev("v_mm")
        s_mm, t_mm, pv_mm = ev("s_mm", H), ev("t_mm", H), ev("pv_mm", CH)
        ot_mm, o2t_mm, proj_mm = ev("ot_mm", TT), ev("o2t_mm"), ev("proj_mm")
        w1_mm, w2_mm = ev("w1_mm", 4, MLP), ev("w2_mm", 1, MLP)
        xt_f, ct_f, x2t_f, ot_f = ev("xt_f"), ev("ct_f", 1, MLP), ev("x2t_f", 1, MLP), ev("ot_f")
        q_done, k_done = ev("q_done"), ev("k_done")
        p_done, pt_even, o_done = ev("p_done", H), ev("pt_even", H // 2), ev("o_done", CH)
        h_done = ev("h_done", 4, MLP)
        setup = sem("setup")
        causal_made, unit_hi, unit_lo = sem("causal_made"), sem("unit_hi"), sem("unit_lo")
        ln_stats, ln_mv, ln_ve, x_hat = ev("ln_stats"), ev("ln_mv"), ev("ln_ve"), ev("x_hat")
        ln2_stats, ln2_mv = ev("ln2_stats", 1, MLP), ev("ln2_mv", 1, MLP)
        ln2_ve, x2_hat_done = ev("ln2_ve", 1, MLP), ev("x2_hat_done", 1, MLP)
        xt_h, ct_h, x2t_h, ot_h = ev("xt_h"), ev("ct_h", 1, MLP), ev("x2t_h", 1, MLP), ev("ot_h")
        q_p1, q_p2, k_p1, k_p2 = ev("q_p1"), ev("q_p2"), ev("k_p1"), ev("k_p2")
        v_done, u_done, pt_odd = ev("v_done"), ev("u_done", H), ev("pt_odd", H // 2)
        bias_done, rden_done, o_norm = ev("bias_done", 1, (0,)), ev("rden_done", TT), ev("o_norm", TT)
        x2_done, h_h, y_done = ev("x2_done"), ev("h_h", 4, MLP), ev("y_done", 1, MLP, credit=1)
        ln_rstd, ln2_rstd = ev("ln_rstd"), ev("ln2_rstd", 1, MLP)
        xt_l, ct_l, x2t_l, ot_l = ev("xt_l"), ev("ct_l", 1, MLP), ev("x2t_l", 1, MLP), ev("ot_l")
        q_r, q_p3, k_r, k_p3 = ev("q_r"), ev("q_p3"), ev("k_r"), ev("k_p3")
        res_done, x2b_done, h_l = ev("res_done", 1, (0,)), ev("x2b_done", 1, MLP), ev("h_l", 4, MLP)

        def has(task, passes=ALL):
            return task is not None and task.p in passes

        def earlier_head(st, h, back):
            return (st.cur, h - back) if h >= back else (st.prev, h - back + H)

        def chunk_at(st, h, lag):
            return (st.cur, (h - lag) // CH) if h >= lag else (st.prev, (h - lag + H) // CH)

        def unit_io(u):
            kind, p, which = UNITS[u]
            if kind == "a":
                a, n = which[0], len(which)
                dram = wa[p, a:a + n].rearrange("w (k p) n -> p (w k) n", p=P)
                st = stage[:, 0:n * KC * D].rearrange("p (w n) -> p w n", n=D)
                return dram, st, *(w[:, a:a + n].rearrange("p w k n -> p (w k) n") for w in (w_hi, w_lo))
            if kind == "w1":
                st = stage[:, :].rearrange("p (k n) -> p k n", k=KC)
                return wm1[p].rearrange("(k p) n -> p k n", p=P), st, w1_hi[:, :, :], w1_lo[:, :, :]
            st = stage[:, :].rearrange("p (k n) -> p k n", k=FT)
            return wm2[p].rearrange("(k p) n -> p k n", p=P), st, w2_hi[:, :, :], w2_lo[:, :, :]

        def unit_users_done(eng, u):
            if u in (4, 8):
                eng.wait_ge(v_mm.sem, v_mm.after(Task(u // 4 - 1, B - 1)))
            if u in (5, 9):
                eng.wait_ge(proj_mm.sem, proj_mm.after(Task(u // 4 - 1, B - 1)))
            if u == 6:
                eng.wait_ge(w1_mm.sem, w1_mm.after(Task(0, B - 1)))
            if u == 7:
                eng.wait_ge(w2_mm.sem, w2_mm.after(Task(0, B - 1)))

        block = es.enter_context(nc.Block())

        @block.sync
        def _(sp):
            sp.dma_start(ident_sb[:, :], ident).then_inc(const_landed, 16)
            sp.dma_start(cols_sb[:, :], cols).then_inc(const_landed, 16)
            sp.dma_start(rows_sb[:, :, :], rows.partition_broadcast(P)).then_inc(const_landed, 16)

            for par in range(2):
                sp.sem_inc(stored.sems[par], 16)

            def source(task):
                return x[task.b] if task.p == 0 else x_mid[task.p - 1, task.b]

            def slot(st, h):
                if st.s is not None:
                    for u in UNIT_AT.get((st.s, h), ()):
                        if u:
                            sp.wait_ge(unit_hi, u)
                            sp.wait_ge(unit_lo, u)
                        dram, place, _, _ = unit_io(u)
                        sp.dma_start(place, dram).then_inc(unit_landed, 16)
                if h == 0 and has(st.nxt, (0,)):
                    if st.prev:
                        sp.wait_ge(u_done.sem, u_done.after(st.prev))
                        sp.sem_inc(passed, 1)
                    sp.dma_start(bias_sb[:, st.nxt.par], tokens(mask[st.nxt.b])).then_inc(mask_landed.of(st.nxt), 16)
                if h == 1 and has(st.nxt2):
                    if st.nxt2.p:
                        writer = Task(st.nxt2.p - 1, st.nxt2.c, st.nxt2.i)
                        sp.wait_ge(stored.of(writer), stored.after(writer))
                        sp.sem_inc(passed, 1)
                    if has(st.cur):
                        sp.wait_ge(xt_mm.sem, xt_mm.after(st.cur))
                        sp.sem_inc(passed, 1)
                    sp.dma_start(x_in[:, st.nxt2.par], tokens(source(st.nxt2))).then_inc(x_landed.of(st.nxt2), 16)
                if h == 2 and has(st.prev):
                    if st.old:
                        sp.wait_ge(x2_done.sem, x2_done.after(st.old))
                        sp.sem_inc(passed, 1)
                    sp.dma_start(x_res[:, :, :], tokens(source(st.prev))).then_inc(res_landed.of(st.prev), 16)
                if h == 5 and has(st.nxt2, (2,)):
                    sp.wait_ge(ct_mm.sem, ct_mm.after(st.nxt if has(st.nxt, (2,)) else Task(0, B - 1)))
                    sp.sem_inc(passed, 1)
                    sp.dma_start(c_in[:, :, :], tokens(ctx[st.nxt2.b])).then_inc(ctx_landed.of(st.nxt2), 16)
                if h == 6 and has(st.nxt):
                    t = st.nxt
                    if st.prev:
                        sp.wait_ge(stacked.of(st.prev), stacked.after(st.prev))
                        sp.sem_inc(passed, 1)
                    sp.wait_ge(q_p2.sem, q_p2.after(t))
                    sp.sem_inc(passed, 1)
                    sp.wait_ge(q_p3.sem, q_p3.after(t))
                    sp.sem_inc(passed, 1)
                    for m in range(KC):
                        sp.dma_start(parts[t.par, 0, :, m * 8:m * 8 + 8].rearrange("j h d s -> (h d) j s"),
                                     q_part[:, :, m, :]).then_inc(q_written.of(t), 16)
                if h == 7 and has(st.nxt):
                    t = st.nxt
                    sp.wait_ge(k_p2.sem, k_p2.after(t))
                    sp.sem_inc(passed, 1)
                    sp.wait_ge(k_p3.sem, k_p3.after(t))
                    sp.sem_inc(passed, 1)
                    for m in range(KC):
                        sp.dma_start(parts[t.par, 1, :, m * 8:m * 8 + 8].rearrange("j h d s -> (h d) j s"),
                                     k_part[:, :, m, :]).then_inc(k_written.of(t), 16)
                    if st.prev:
                        sp.wait_ge(s_mm.sem, s_mm.after(st.prev))
                        sp.sem_inc(passed, 1)
                    sp.wait_ge(q_written.of(t), q_written.after(t))
                    sp.sem_inc(passed, 1)
                    for j, part in enumerate(Q_PARTS):
                        sp.dma_start(q_stack[j * HD:(j + 1) * HD, t.par],
                                     parts[t.par, 0, part].rearrange("h d s -> d h s")).then_inc(stacked.of(t), 16)
                    sp.wait_ge(k_written.of(t), k_written.after(t))
                    sp.sem_inc(passed, 1)
                    for j, part in enumerate(K_PARTS):
                        sp.dma_start(k_stack[j * HD:(j + 1) * HD, t.par],
                                     parts[t.par, 1, part].rearrange("h d s -> d h s")).then_inc(stacked.of(t), 16)
                if h == 12 and has(st.cur, (0,)):
                    if st.prev:
                        sp.wait_ge(ct_mm.sem, ct_mm.after(st.prev))
                        sp.sem_inc(passed, 1)
                    sp.dma_start(c_in[:, :, :], tokens(ctx[st.cur.b])).then_inc(ctx_landed.of(st.cur), 16)
                if h == 15 and has(st.prev, (1,)):
                    sp.wait_ge(x2_done.sem, x2_done.after(st.prev))
                    sp.sem_inc(passed, 1)
                    sp.dma_start(tokens(x_mid[1, st.prev.b]), x2[:, st.prev.par]).then_inc(stored.of(st.prev), 16)
                if h == 15 and has(st.old, MLP):
                    sp.wait_ge(y_done.sem, y_done.after(st.old))
                    sp.sem_inc(passed, 1)
                    dst = x_mid[0, st.old.b] if st.old.p == 0 else out[st.old.b]
                    sp.dma_start(tokens(dst), y_sb[:, :, :]).then_inc(stored.of(st.old), 16)

            steps(sp, lambda st: [slot(st, h) for h in range(H)])
            for b in (B - 2, B - 1):
                sp.wait_ge(stored.of(Task(NPASS - 1, b)), stored.after(Task(NPASS - 1, b)))
                sp.sem_inc(passed, 1)

        @block.tensor
        def _(pe):
            mm = nc.tensor.matmul
            pe.wait_ge(const_landed, 48)
            pe.wait_ge(setup, 3)

            def product(dst, pairs):
                terms = [t for lh, ll, rh, rl in pairs for t in ((lh, rh), (lh, rl), (ll, rh))]
                for n, (lhs, rhs) in enumerate(terms):
                    last = mm(dst, lhs, rhs, start=(n == 0), stop=(n == len(terms) - 1))
                return last

            def flip(dst, src):
                for k in range(KC):
                    for t in range(TT):
                        last = nc.tensor.transpose(dst[:, k * S + t * P:k * S + (t + 1) * P],
                                                   src[:, t, k * P:(k + 1) * P], ident_sb[:, :])
                return last

            def features(bank, w, src_hi, src_lo):
                for m in range(KC):
                    c = slice(m * P, (m + 1) * P)
                    last = product(d_ps[:, bank, m * S:(m + 1) * S],
                                   [(w_hi[:, w, k, c], w_lo[:, w, k, c], src_hi[:, k, :], src_lo[:, k, :])
                                    for k in range(KC)])
                return last

            def by_token(bank, sources):
                for t in range(TT):
                    c = slice(t * P, (t + 1) * P)
                    last = product(d_ps[:, bank, t * D:(t + 1) * D],
                                   [(a_hi[:, k, c], a_lo[:, k, c], w_hi[:, w, k, :], w_lo[:, w, k, :])
                                    for a_hi, a_lo, w in sources for k in range(KC)])
                return last

            def weights(task, units):
                if task.first:
                    pe.wait_ge(unit_hi, units[task.p] + 1)
                    pe.wait_ge(unit_lo, units[task.p] + 1)

            def scores(st, h):
                t = st.cur
                if h == 0:
                    pe.wait_ge(stacked.of(t), stacked.after(t))
                before, hb = earlier_head(st, h, 2)
                if has(before, (2,)):
                    pe.wait_ge(p_done.sem, p_done.after(before, hb + 1))
                elif before:
                    pe.wait_ge(u_done.sem, u_done.after(before, hb + 1))
                for q in range(TT):
                    n = (q + 1) * P if t.p == 1 else S
                    last = mm(s_ps[:, h % 2, q * S:q * S + n], q_stack[:, t.par, h, q * P:(q + 1) * P],
                              k_stack[:, t.par, h, 0:n], start=True, stop=True)
                last.then_inc(s_mm.sem, 1)

            def transposed_probs(t, h, st):
                pe.wait_ge(p_done.sem, p_done.after(t, h + 1))
                before, hb = (t, h - 2) if h >= 2 else (st.prev if t is st.cur else st.old, h + H - 2)
                if before and h % 2:
                    pe.wait_ge(pt_odd.sem, pt_odd.after(before, hb // 2 + 1))
                elif before:
                    pe.wait_ge(pt_even.sem, pt_even.after(before, hb // 2 + 1))
                for k in range(TT):
                    for q in range(TT):
                        if t.p == 1 and k > q:
                            continue
                        c = k * S + (q * P if not (t.p == 1 and k) else 0)
                        last = nc.tensor.transpose(t_ps[:, h % 2, c:c + P],
                                                   prob[:, h % 4, q, k * P:(k + 1) * P], ident_sb[:, :])
                last.then_inc(t_mm.sem, 1)

            def values(st, t, c):
                if c == 0:
                    pe.wait_ge(v_done.sem, v_done.after(t))
                    before = st.prev
                else:
                    before = t
                pe.wait_ge(pt_even.sem, pt_even.after(t, 2 * c + 2))
                pe.wait_ge(pt_odd.sem, pt_odd.after(t, 2 * c + 2))
                if before:
                    pe.wait_ge(o_done.sem, o_done.after(before, (c - 1) % CH + 1))
                for k in range(TT):
                    lo = P if (t.p == 1 and k) else 0
                    for j in range(CH):
                        h = CH * c + j
                        last = mm(o_ps[32 * j:32 * j + VW, lo:S], v_sb[:, t.par, k, h, :],
                                  prob_t[:, h % 8, k * S:k * S + S - lo], start=(k == 0), stop=(k == TT - 1),
                                  tile_position=(0, 32 * j))
                last.then_inc(pv_mm.sem, 1)

            def head_tokens(st, q):
                t = st.prev
                if q == 0:
                    pe.wait_ge(o_done.sem, o_done.after(t))
                    if has(t, (0,)):
                        pe.wait_ge(ct_f.sem, ct_f.after(t))
                    elif has(st.old, MLP):
                        pe.wait_ge(x2t_f.sem, x2t_f.after(st.old))
                    if st.nxt:
                        pe.wait_ge(xt_f.sem, xt_f.after(st.nxt))
                    if st.old:
                        pe.wait_ge(ot_f.sem, ot_f.after(st.old))
                else:
                    pe.wait_ge(o_norm.sem, o_norm.after(t, 1))
                for c in range(CH):
                    last = nc.tensor.transpose(m_ps[:, c * P:(c + 1) * P], o_t[:, c, q * P:(q + 1) * P],
                                               ident_sb[:, :])
                last.then_inc(ot_mm.sem, 1)

            def slot(st, h):
                if has(st.cur):
                    scores(st, h)
                t, ht = earlier_head(st, h, 2)
                if t is not None:
                    transposed_probs(t, ht, st)
                if h == 0 and has(st.nxt):
                    pe.wait_ge(x_hat.sem, x_hat.after(st.nxt))
                    if st.old:
                        pe.wait_ge(ot_f.sem, ot_f.after(st.old))
                    if st.old is None:
                        if st.cur:
                            pe.wait_ge(xt_f.sem, xt_f.after(st.cur))
                    if has(st.nxt, (2,)):
                        pe.wait_ge(ct_f.sem, ct_f.after(st.nxt))
                    flip(m_ps, x_in[:, st.nxt.par]).then_inc(xt_mm.sem, 1)
                if h == 1 and has(st.old, MLP):
                    pe.wait_ge(x2_hat_done.sem, x2_hat_done.after(st.old))
                    if st.nxt:
                        pe.wait_ge(xt_f.sem, xt_f.after(st.nxt))
                    pe.wait_ge(ot_f.sem, ot_f.after(st.old))
                    flip(m_ps, x2_hat).then_inc(x2t_mm.sem, 1)
                if h == 2 and has(st.nxt):
                    weights(st.nxt, UNIT_QKV)
                    pe.wait_ge(xt_h.sem, xt_h.after(st.nxt))
                    pe.wait_ge(xt_l.sem, xt_l.after(st.nxt))
                    if st.cur:
                        pe.wait_ge(v_done.sem, v_done.after(st.cur))
                    if st.older:
                        pe.wait_ge(y_done.sem, y_done.after(st.older))
                    features(0, WQ, xt_hi, xt_lo).then_inc(q_mm.sem, 1)
                kv = (ct_hi, ct_lo) if has(st.nxt, (2,)) else (xt_hi, xt_lo)
                if h == 3 and has(st.nxt):
                    if has(st.nxt, (2,)):
                        pe.wait_ge(ct_h.sem, ct_h.after(st.nxt))
                        pe.wait_ge(ct_l.sem, ct_l.after(st.nxt))
                    if st.cur:
                        pe.wait_ge(k_done.sem, k_done.after(st.cur))
                    if st.old:
                        pe.wait_ge(x2_done.sem, x2_done.after(st.old))
                    features(1, WK, *kv).then_inc(k_mm.sem, 1)
                if h == 4 and has(st.nxt):
                    pe.wait_ge(q_done.sem, q_done.after(st.nxt))
                    by_token(0, [(*kv, WV)]).then_inc(v_mm.sem, 1)
                if h == 4 and has(st.prev, (0,)):
                    pe.wait_ge(ctx_landed.of(st.prev), ctx_landed.after(st.prev))
                    if st.old:
                        pe.wait_ge(x2t_f.sem, x2t_f.after(st.old))
                    if st.nxt:
                        pe.wait_ge(xt_f.sem, xt_f.after(st.nxt))
                    if st.old:
                        pe.wait_ge(ot_f.sem, ot_f.after(st.old))
                    flip(m_ps, c_in).then_inc(ct_mm.sem, 1)
                if 5 <= h <= 8 and has(st.old, MLP):
                    n = h - 5
                    if n == 0:
                        weights(st.old, UNIT_W1)
                        pe.wait_ge(x2t_h.sem, x2t_h.after(st.old))
                        pe.wait_ge(x2t_l.sem, x2t_l.after(st.old))
                        if st.nxt:
                            pe.wait_ge(k_done.sem, k_done.after(st.nxt))
                        pe.wait_ge(x2_done.sem, x2_done.after(st.old))
                    elif n == 1:
                        if st.nxt:
                            pe.wait_ge(v_done.sem, v_done.after(st.nxt))
                        if st.older:
                            pe.wait_ge(y_done.sem, y_done.after(st.older))
                    else:
                        pe.wait_ge(h_done.sem, h_done.after(st.old, n - 1))
                    for f in range(2):
                        c = slice((2 * n + f) * P, (2 * n + f + 1) * P)
                        last = product(d_ps[:, 1 - n % 2, f * S:(f + 1) * S],
                                       [(w1_hi[:, k, c], w1_lo[:, k, c], x2t_hi[:, k, :], x2t_lo[:, k, :])
                                        for k in range(KC)])
                    last.then_inc(w1_mm.sem, 1)
                if h in (6, 7) and has(st.prev):
                    head_tokens(st, h - 6)
                if h == 9 and has(st.prev):
                    pe.wait_ge(o_norm.sem, o_norm.after(st.prev))
                    flip(m_ps, o_sb).then_inc(o2t_mm.sem, 1)
                if h == 11 and has(st.nxt2, (2,)):
                    pe.wait_ge(ctx_landed.of(st.nxt2), ctx_landed.after(st.nxt2))
                    if st.nxt:
                        pe.wait_ge(xt_f.sem, xt_f.after(st.nxt))
                    if st.prev:
                        pe.wait_ge(ot_f.sem, ot_f.after(st.prev))
                    if st.old:
                        pe.wait_ge(x2t_f.sem, x2t_f.after(st.old))
                    flip(m_ps, c_in).then_inc(ct_mm.sem, 1)
                if h == 12 and has(st.prev):
                    t = st.prev
                    weights(t, UNIT_O)
                    pe.wait_ge(ot_h.sem, ot_h.after(t))
                    pe.wait_ge(ot_l.sem, ot_l.after(t))
                    if st.nxt:
                        pe.wait_ge(k_done.sem, k_done.after(st.nxt))
                    if st.old:
                        pe.wait_ge(x2_done.sem, x2_done.after(st.old))
                    if has(st.old, MLP):
                        pe.wait_ge(h_done.sem, h_done.after(st.old, 3))
                    src = [(ot_hi, ot_lo, WO)]
                    if t.p == 0:
                        pe.wait_ge(ct_h.sem, ct_h.after(t))
                        pe.wait_ge(ct_l.sem, ct_l.after(t))
                        src.append((ct_hi, ct_lo, WG))
                    by_token(1, src).then_inc(proj_mm.sem, 1)
                if h == 13 and has(st.old, MLP):
                    weights(st.old, UNIT_W2)
                    pe.wait_ge(h_h.sem, h_h.after(st.old))
                    pe.wait_ge(h_l.sem, h_l.after(st.old))
                    for t in range(TT):
                        c = slice(t * P, (t + 1) * P)
                        last = product(d_ps[:, 0, t * D:(t + 1) * D],
                                       [(h_hi[:, f, c], h_lo[:, f, c], w2_hi[:, f, :], w2_lo[:, f, :])
                                        for f in range(FT)])
                    last.then_inc(w2_mm.sem, 1)
                if h % CH == 3:
                    t, c = chunk_at(st, h, 7)
                    if t is not None:
                        values(st, t, c)

            steps(pe, lambda st: [slot(st, h) for h in range(H)])

        @block.scalar
        def _(act):
            act.wait_ge(const_landed, 48)
            act.wait_ge(setup, 2)

            def probs(st, h):
                t = st.cur
                act.wait_ge(u_done.sem, u_done.after(t, h + 1))
                if t.p == 2:
                    before, hb = earlier_head(st, h, 4)
                    if before:
                        act.wait_ge(t_mm.sem, t_mm.after(before, hb + 1))
                for q in range(TT):
                    n = (q + 1) * P if t.p == 1 else S
                    src = s_ps[:, h % 2, q * S:q * S + n] if t.p == 2 else prob[:, h % 4, q, 0:n]
                    last = nc.scalar.activation(prob[:, h % 4, q, 0:n], src, ACT.Exp,
                                                bias=neg_max[:, h % 4, q:q + 1], scale=-1.0)
                last.then_inc(p_done.sem, 1)

            def affine(dst, col_g, col_b, done):
                for k in range(KC):
                    last = nc.scalar.activation(dst[:, k, :], m_ps[:, k * S:(k + 1) * S], ACT.Identity,
                                                bias=cols_sb[:, col_b + k:col_b + k + 1],
                                                scale=cols_sb[:, col_g + k:col_g + k + 1])
                last.then_inc(done.sem, 1)

            def slot(st, h):
                if h == 1 and has(st.nxt):
                    act.wait_ge(xt_mm.sem, xt_mm.after(st.nxt))
                    if st.old:
                        act.wait_ge(ot_h.sem, ot_h.after(st.old))
                        act.wait_ge(ot_l.sem, ot_l.after(st.old))
                    if st.old is None:
                        if st.cur:
                            act.wait_ge(xt_h.sem, xt_h.after(st.cur))
                            act.wait_ge(xt_l.sem, xt_l.after(st.cur))
                    c = C_LN + 4 * st.nxt.p
                    affine(tf_a, c, c + 2, xt_f)
                if has(st.cur):
                    probs(st, h)
                t, ht = earlier_head(st, h, 2)
                if t is not None and ht % 2 == 0:
                    act.wait_ge(t_mm.sem, t_mm.after(t, ht + 1))
                    back = (t, ht - 8) if ht >= 8 else (st.prev if t is st.cur else st.old, ht + 8)
                    if back[0]:
                        act.wait_ge(pv_mm.sem, pv_mm.after(back[0], back[1] // CH + 1))
                    n = 384 if t.p == 1 else 512
                    nc.scalar.activation(prob_t[:, ht % 8, 0:n], t_ps[:, 0, 0:n], ACT.Copy).then_inc(pt_even.sem, 1)
                if h % CH == 0:
                    t, c = chunk_at(st, h, 8)
                    if t is not None:
                        act.wait_ge(pv_mm.sem, pv_mm.after(t, c + 1))
                        if c == 0:
                            if st.prev:
                                act.wait_ge(ot_mm.sem, ot_mm.after(st.prev))
                        nc.scalar.activation(o_t[:, c, :], o_ps[:, 0:S], ACT.Copy).then_inc(o_done.sem, 1)
                if h == 2 and has(st.old, MLP):
                    act.wait_ge(x2t_mm.sem, x2t_mm.after(st.old))
                    if has(st.old, (0,)):
                        act.wait_ge(ct_h.sem, ct_h.after(st.old))
                        act.wait_ge(ct_l.sem, ct_l.after(st.old))
                    else:
                        if st.nxt:
                            act.wait_ge(ct_h.sem, ct_h.after(st.nxt))
                            act.wait_ge(ct_l.sem, ct_l.after(st.nxt))
                    c = C_LN2 + 4 * MLP.index(st.old.p)
                    affine(tf_b, c, c + 2, x2t_f)
                if h == 3 and has(st.nxt):
                    act.wait_ge(q_mm.sem, q_mm.after(st.nxt))
                    if st.cur:
                        act.wait_ge(q_p3.sem, q_p3.after(st.cur))
                    if st.nxt.p == 0:
                        for m in range(KC):
                            last = nc.scalar.activation(q_f[:, m, :], d_ps[:, 0, m * S:(m + 1) * S], ACT.Identity,
                                                        bias=cols_sb[:, C_BQ + m:C_BQ + m + 1], scale=-0.25)
                    else:
                        last = nc.scalar.activation(q_f[:, :, :], d_ps[:, 0, :].rearrange("p (m s) -> p m s", m=KC),
                                                    ACT.Copy, scale=-0.25)
                    last.then_inc(q_done.sem, 1)
                if h == 4 and has(st.nxt):
                    act.wait_ge(k_mm.sem, k_mm.after(st.nxt))
                    if st.cur:
                        act.wait_ge(k_p3.sem, k_p3.after(st.cur))
                    if st.nxt.p == 0:
                        for m in range(KC):
                            last = nc.scalar.activation(k_f[:, m, :], d_ps[:, 1, m * S:(m + 1) * S], ACT.Identity,
                                                        bias=cols_sb[:, C_BK + m:C_BK + m + 1])
                    else:
                        last = nc.scalar.activation(k_f[:, :, :], d_ps[:, 1, :].rearrange("p (m s) -> p m s", m=KC),
                                                    ACT.Copy)
                    last.then_inc(k_done.sem, 1)
                if h == 5 and has(st.prev, (0,)):
                    act.wait_ge(ct_mm.sem, ct_mm.after(st.prev))
                    if st.old:
                        act.wait_ge(x2t_h.sem, x2t_h.after(st.old))
                        act.wait_ge(x2t_l.sem, x2t_l.after(st.old))
                        act.wait_ge(ct_l.sem, ct_l.after(st.old))
                    nc.scalar.activation(tf_b[:, :, :], m_ps[:, :].rearrange("p (k s) -> p k s", k=KC), ACT.Copy)\
                        .then_inc(ct_f.sem, 1)
                if 6 <= h <= 9 and has(st.old, MLP):
                    n = h - 6
                    act.wait_ge(w1_mm.sem, w1_mm.after(st.old, n + 1))
                    if n >= 2:
                        act.wait_ge(h_h.sem, h_h.after(st.old, n - 1))
                        act.wait_ge(h_l.sem, h_l.after(st.old, n - 1))
                    for f in range(2):
                        c = C_B1 + FT * MLP.index(st.old.p) + 2 * n + f
                        last = nc.scalar.activation(h_f[:, n % 2, f, :], d_ps[:, 1 - n % 2, f * S:(f + 1) * S], ACT.Relu,
                                                    bias=cols_sb[:, c:c + 1])
                    last.then_inc(h_done.sem, 1)
                if h == 10 and has(st.prev):
                    act.wait_ge(o2t_mm.sem, o2t_mm.after(st.prev))
                    if st.nxt:
                        act.wait_ge(xt_h.sem, xt_h.after(st.nxt))
                        act.wait_ge(xt_l.sem, xt_l.after(st.nxt))
                    if st.old:
                        act.wait_ge(ot_l.sem, ot_l.after(st.old))
                    nc.scalar.activation(tf_a[:, :, :], m_ps[:, :].rearrange("p (k s) -> p k s", k=KC), ACT.Copy)\
                        .then_inc(ot_f.sem, 1)
                if h == 12 and has(st.nxt2, (2,)):
                    act.wait_ge(ct_mm.sem, ct_mm.after(st.nxt2))
                    if st.old:
                        act.wait_ge(x2t_h.sem, x2t_h.after(st.old))
                        act.wait_ge(x2t_l.sem, x2t_l.after(st.old))
                    if has(st.nxt, (2,)):
                        act.wait_ge(ct_h.sem, ct_h.after(st.nxt))
                        act.wait_ge(ct_l.sem, ct_l.after(st.nxt))
                    nc.scalar.activation(tf_b[:, :, :], m_ps[:, :].rearrange("p (k s) -> p k s", k=KC), ACT.Copy)\
                        .then_inc(ct_f.sem, 1)

            steps(act, lambda st: [slot(st, h) for h in range(H)])

        @block.vector
        def _(dve):
            v = nc.vector
            v.memset(o_ps[:, :], 0.0).then_inc(setup, 1)
            dve.wait_ge(const_landed, 48)
            v.tensor_scalar(cols_sb[:, C_BQ:C_BQ + KC], cols_sb[:, C_BQ:C_BQ + KC], -0.25, None, ALU.mult)\
                .then_inc(setup, 1)
            v.memset(v_sb[:, :, :, :, HD:VW], 1.0).then_inc(setup, 1)

            def score_guard(st, h):
                t = st.cur
                dve.wait_ge(s_mm.sem, s_mm.after(t, h + 1))
                before, hb = earlier_head(st, h, 4)
                if t.p == 2:
                    if before:
                        dve.wait_ge(p_done.sem, p_done.after(before, hb + 1))
                    v.tensor_reduce(neg_max[:, h % 4, :], s_ps[:, h % 2, :].rearrange("p (q k) -> p q k", q=TT),
                                    AX_X, ALU.min).then_inc(u_done.sem, 1)
                    return
                if before:
                    dve.wait_ge(t_mm.sem, t_mm.after(before, hb + 1))
                if h == 0 and t.p == 0:
                    dve.wait_ge(bias_done.sem, bias_done.after(t))
                if h == 0 and t.first and t.p == 1:
                    dve.wait_ge(causal_made, 3)
                dve.sem_inc(passed, 1)
                for q in range(TT):
                    n = (q + 1) * P if t.p == 1 else S
                    bias = causal[:, q, 0:n] if t.p == 1 else bias_sb[:, t.par, q, 0:n]
                    last = v.tensor_tensor_reduce(prob[:, h % 4, q, 0:n], s_ps[:, h % 2, q * S:q * S + n], bias,
                                                  1.0, HUGE, ALU.add, ALU.min, neg_max[:, h % 4, q:q + 1])
                last.then_inc(u_done.sem, 1)

            def statistics(src, st_t, done):
                for t in range(TT):
                    last = v.bn_stats(st_t[:, t, :], src[:, t, :])
                last.then_inc(done.sem, 1)

            def aggregate(task, st_t, mv_t, ve_t, eps, stats_done, mv_done, ve_done):
                dve.wait_ge(stats_done.sem, stats_done.after(task))
                dve.sem_inc(passed, 1)
                for t in range(TT):
                    last = v.bn_aggr(mv_t[:, t, :], st_t[:, t, :])
                last.then_inc(mv_done.sem, 1)
                dve.wait_ge(mv_done.sem, mv_done.after(task))
                v.tensor_scalar(ve_t[:, :], mv_t[:, :, 1], eps, None, ALU.add).then_inc(ve_done.sem, 1)

            def normalise(dst, src, mv_t, rstd_t, done):
                for t in range(TT):
                    last = v.tensor_scalar(dst[:, t, :], src[:, t, :], mv_t[:, t, 0:1], rstd_t[:, t:t + 1],
                                           ALU.subtract, ALU.mult)
                last.then_inc(done.sem, 1)

            def slot(st, h):
                if has(st.cur):
                    score_guard(st, h)
                t, ht = earlier_head(st, h, 2)
                if t is not None and ht % 2:
                    dve.wait_ge(t_mm.sem, t_mm.after(t, ht + 1))
                    back = (t, ht - 8) if ht >= 8 else (st.prev if t is st.cur else st.old, ht + 8)
                    if back[0]:
                        dve.wait_ge(pv_mm.sem, pv_mm.after(back[0], back[1] // CH + 1))
                    n = 384 if t.p == 1 else 512
                    v.tensor_copy(prob_t[:, ht % 8, 0:n], t_ps[:, 1, 0:n]).then_inc(pt_odd.sem, 1)
                if h == 1 and has(st.nxt):
                    dve.wait_ge(xt_f.sem, xt_f.after(st.nxt))
                    if st.cur:
                        dve.wait_ge(v_mm.sem, v_mm.after(st.cur))
                    v.tensor_copy(xt_hi[:, :, :], tf_a[:, :, :]).then_inc(xt_h.sem, 1)
                if h == 3 and has(st.old, MLP):
                    dve.wait_ge(x2t_f.sem, x2t_f.after(st.old))
                    v.tensor_copy(x2t_hi[:, :, :], tf_b[:, :, :]).then_inc(x2t_h.sem, 1)
                if h == 3 and has(st.nxt, (0,)):
                    dve.wait_ge(mask_landed.of(st.nxt), mask_landed.after(st.nxt))
                    v.tensor_scalar(bias_sb[:, st.nxt.par], bias_sb[:, st.nxt.par], 1.0, -MASKED,
                                    ALU.subtract, ALU.mult).then_inc(bias_done.sem, 1)
                if h == 4 and has(st.nxt):
                    dve.wait_ge(q_done.sem, q_done.after(st.nxt))
                    if st.cur:
                        dve.wait_ge(q_written.of(st.cur), q_written.after(st.cur))
                    v.tensor_copy(q_part[:, 0], q_f[:, :, :]).then_inc(q_p1.sem, 1)
                if h == 5 and has(st.nxt):
                    dve.wait_ge(k_done.sem, k_done.after(st.nxt))
                    if st.cur:
                        dve.wait_ge(k_written.of(st.cur), k_written.after(st.cur))
                    v.tensor_copy(k_part[:, 0], k_f[:, :, :]).then_inc(k_p1.sem, 1)
                    dve.wait_ge(q_r.sem, q_r.after(st.nxt))
                    v.tensor_copy(q_part[:, 1], q_f[:, :, :]).then_inc(q_p2.sem, 1)
                    dve.wait_ge(v_mm.sem, v_mm.after(st.nxt))
                    if st.prev:
                        dve.wait_ge(pv_mm.sem, pv_mm.after(st.prev))
                    for k in range(TT):
                        dst = v_sb[:, st.nxt.par, k, :, 0:HD]
                        src = d_ps[:, 0, k * D:(k + 1) * D].rearrange("p (h d) -> p h d", d=HD)
                        if st.nxt.p == 0:
                            bv = rows_sb[:, R_BV, :].rearrange("p (h d) -> p h d", d=HD)
                            last = v.tensor_tensor(dst, src, bv, ALU.add)
                        else:
                            last = v.tensor_copy(dst, src)
                    last.then_inc(v_done.sem, 1)
                if h == 6 and has(st.nxt):
                    dve.wait_ge(k_r.sem, k_r.after(st.nxt))
                    v.tensor_copy(k_part[:, 1], k_f[:, :, :]).then_inc(k_p2.sem, 1)
                if h == 6 and has(st.prev, (0,)):
                    dve.wait_ge(ct_f.sem, ct_f.after(st.prev))
                    if st.old:
                        dve.wait_ge(proj_mm.sem, proj_mm.after(st.old))
                    v.tensor_copy(ct_hi[:, :, :], tf_b[:, :, :]).then_inc(ct_h.sem, 1)
                if 7 <= h <= 10 and has(st.old, MLP):
                    n = h - 7
                    dve.wait_ge(h_done.sem, h_done.after(st.old, n + 1))
                    v.tensor_copy(h_hi[:, 2 * n:2 * n + 2, :], h_f[:, n % 2]).then_inc(h_h.sem, 1)
                if h in (7, 8) and has(st.prev):
                    q = h - 7
                    dve.wait_ge(ot_mm.sem, ot_mm.after(st.prev, q + 1))
                    if st.old:
                        dve.wait_ge(o2t_mm.sem, o2t_mm.after(st.old))
                    o = m_ps[:, :].rearrange("p (h w) -> p h w", w=32)
                    v.reciprocal(rden[:, q, :], o[:, :, HD]).then_inc(rden_done.sem, 1)
                    dve.wait_ge(rden_done.sem, rden_done.after(st.prev, q + 1))
                    v.tensor_tensor(o_sb[:, q, :].rearrange("p (h d) -> p h d", d=HD), o[:, :, 0:HD],
                                    rden[:, q, :].unsqueeze(2).to_broadcast([P, H, HD]), ALU.mult)\
                        .then_inc(o_norm.sem, 1)
                if h == 11 and has(st.prev):
                    dve.wait_ge(ot_f.sem, ot_f.after(st.prev))
                    if st.old:
                        dve.wait_ge(proj_mm.sem, proj_mm.after(st.old))
                    v.tensor_copy(ot_hi[:, :, :], tf_a[:, :, :]).then_inc(ot_h.sem, 1)
                if h == 12 and has(st.nxt2):
                    dve.wait_ge(x_landed.of(st.nxt2), x_landed.after(st.nxt2))
                    if st.nxt:
                        dve.wait_ge(ln_mv.sem, ln_mv.after(st.nxt))
                    statistics(x_in[:, st.nxt2.par], stats, ln_stats)
                if h == 13 and has(st.nxt2):
                    if st.nxt:
                        dve.wait_ge(x_hat.sem, x_hat.after(st.nxt))
                        dve.wait_ge(ln_rstd.sem, ln_rstd.after(st.nxt))
                    aggregate(st.nxt2, stats, mv, ve, LN_EPS[st.nxt2.p], ln_stats, ln_mv, ln_ve)
                if h == 13 and has(st.nxt2, (2,)):
                    dve.wait_ge(ct_f.sem, ct_f.after(st.nxt2))
                    if st.nxt:
                        dve.wait_ge(v_mm.sem, v_mm.after(st.nxt))
                    v.tensor_copy(ct_hi[:, :, :], tf_b[:, :, :]).then_inc(ct_h.sem, 1)
                if h == 13 and has(st.prev):
                    t = st.prev
                    dve.wait_ge(proj_mm.sem, proj_mm.after(t))
                    if t.p == 0:
                        dve.wait_ge(res_done.sem, res_done.after(t))
                    else:
                        dve.wait_ge(res_landed.of(t), res_landed.after(t))
                    if st.older:
                        dve.wait_ge(stored.of(st.older), stored.after(st.older))
                    v.tensor_tensor(x2[:, t.par], d_ps[:, 1, :].rearrange("p (t d) -> p t d", t=TT),
                                    x_res[:, :, :], ALU.add).then_inc(x2_done.sem, 1)
                if h == 14 and has(st.prev, MLP):
                    t = st.prev
                    dve.wait_ge(x2_done.sem, x2_done.after(t))
                    if st.old:
                        dve.wait_ge(ln2_mv.sem, ln2_mv.after(st.old))
                    statistics(x2[:, t.par], stats2, ln2_stats)
                    if st.old:
                        dve.wait_ge(x2_hat_done.sem, x2_hat_done.after(st.old))
                        dve.wait_ge(ln2_rstd.sem, ln2_rstd.after(st.old))
                    aggregate(t, stats2, mv2, ve2, LN_EPS[t.p], ln2_stats, ln2_mv, ln2_ve)
                if h == 14 and has(st.old, MLP):
                    dve.wait_ge(w2_mm.sem, w2_mm.after(st.old))
                    dve.wait_ge(x2b_done.sem, x2b_done.after(st.old))
                    if st.older:
                        dve.wait_ge(stored.of(st.older), stored.after(st.older))
                    v.tensor_tensor(y_sb[:, :, :], d_ps[:, 0, :].rearrange("p (t d) -> p t d", t=TT),
                                    x2[:, st.old.par], ALU.add).then_inc(y_done.sem, 1)
                if h == 15 and has(st.nxt2):
                    dve.wait_ge(ln_rstd.sem, ln_rstd.after(st.nxt2))
                    normalise(x_in[:, st.nxt2.par], x_in[:, st.nxt2.par], mv, rstd, x_hat)
                if h == 15 and has(st.prev, MLP):
                    dve.wait_ge(ln2_rstd.sem, ln2_rstd.after(st.prev))
                    if st.old:
                        dve.wait_ge(x2t_mm.sem, x2t_mm.after(st.old))
                    normalise(x2_hat, x2[:, st.prev.par], mv2, rstd2, x2_hat_done)
                if st.s is not None:
                    for u in UNIT_AT.get((st.s, h), ()):
                        dve.wait_ge(unit_landed, 16 * (u + 1))
                        unit_users_done(dve, u)
                        _, place, hi, _ = unit_io(u)
                        v.tensor_copy(hi, place).then_inc(unit_hi, 1)

            dve.sem_inc(y_done.sem, 1)
            steps(dve, lambda st: [slot(st, h) for h in range(H)])

        @block.gpsimd
        def _(pool):
            g = nc.gpsimd
            g.memset(minus_half[:, :], -0.5).then_inc(causal_made, 1)
            g.memset(causal[:, :, :], 0.0).then_inc(causal_made, 1)
            pool.wait_ge(causal_made, 2)
            g.affine_select(out=causal[:, :, :], in_=causal[:, :, :], compare_op=ALU.is_ge, fill=MASKED, base=0,
                            pattern=[[P, TT], [-1, S]], channel_multiplier=1).then_inc(causal_made, 1)
            pool.wait_ge(const_landed, 48)
            g.tensor_tensor(rows_sb[:, R_BO, :], rows_sb[:, R_BO, :], rows_sb[:, R_BG, :], ALU.add)\
                .then_inc(causal_made, 1)
            pool.wait_ge(causal_made, 4)

            def sub(dst, a, b, done):
                if b.dtype == F32R:
                    b = b.bitcast(F32)
                g.tensor_tensor(dst, a, b, ALU.subtract).then_inc(done, 1)

            def per_token(row):
                return rows_sb[:, row, :].unsqueeze(1).to_broadcast([P, TT, D])

            def slot(st, h):
                if h == 1 and has(st.nxt):
                    pool.wait_ge(xt_h.sem, xt_h.after(st.nxt))
                    sub(xt_lo[:, :, :], tf_a[:, :, :], xt_hi[:, :, :], xt_l.sem)
                if h == 3 and has(st.old, MLP):
                    pool.wait_ge(x2t_h.sem, x2t_h.after(st.old))
                    sub(x2t_lo[:, :, :], tf_b[:, :, :], x2t_hi[:, :, :], x2t_l.sem)
                if h == 4 and has(st.nxt):
                    pool.wait_ge(q_p1.sem, q_p1.after(st.nxt))
                    sub(q_f[:, :, :], q_f[:, :, :], q_part[:, 0], q_r.sem)
                if h == 5 and has(st.nxt):
                    pool.wait_ge(k_p1.sem, k_p1.after(st.nxt))
                    sub(k_f[:, :, :], k_f[:, :, :], k_part[:, 0], k_r.sem)
                    pool.wait_ge(q_p2.sem, q_p2.after(st.nxt))
                    sub(q_part[:, 2], q_f[:, :, :], q_part[:, 1], q_p3.sem)
                if h == 6 and has(st.nxt):
                    pool.wait_ge(k_p2.sem, k_p2.after(st.nxt))
                    sub(k_part[:, 2], k_f[:, :, :], k_part[:, 1], k_p3.sem)
                if h == 6 and has(st.prev, (0,)):
                    pool.wait_ge(ct_h.sem, ct_h.after(st.prev))
                    sub(ct_lo[:, :, :], tf_b[:, :, :], ct_hi[:, :, :], ct_l.sem)
                if 7 <= h <= 10 and has(st.old, MLP):
                    n = h - 7
                    pool.wait_ge(h_h.sem, h_h.after(st.old, n + 1))
                    sub(h_lo[:, 2 * n:2 * n + 2, :], h_f[:, n % 2], h_hi[:, 2 * n:2 * n + 2, :], h_l.sem)
                if h == 10 and has(st.prev, (0,)):
                    pool.wait_ge(res_landed.of(st.prev), res_landed.after(st.prev))
                    g.tensor_tensor(x_res[:, :, :], x_res[:, :, :], per_token(R_BO), ALU.add).then_inc(res_done.sem, 1)
                if h == 11 and has(st.prev):
                    pool.wait_ge(ot_h.sem, ot_h.after(st.prev))
                    sub(ot_lo[:, :, :], tf_a[:, :, :], ot_hi[:, :, :], ot_l.sem)
                if h == 12 and has(st.old, MLP):
                    pool.wait_ge(x2_hat_done.sem, x2_hat_done.after(st.old))
                    r = R_B2 + MLP.index(st.old.p)
                    g.tensor_tensor(x2[:, st.old.par], x2[:, st.old.par], per_token(r), ALU.add)\
                        .then_inc(x2b_done.sem, 1)
                if h == 13 and has(st.nxt2):
                    pool.wait_ge(ln_ve.sem, ln_ve.after(st.nxt2))
                    if st.nxt:
                        pool.wait_ge(x_hat.sem, x_hat.after(st.nxt))
                    g.tensor_tensor(rstd[:, :], ve[:, :], minus_half[:, :], ALU.pow).then_inc(ln_rstd.sem, 1)
                if h == 13 and has(st.nxt2, (2,)):
                    pool.wait_ge(ct_h.sem, ct_h.after(st.nxt2))
                    sub(ct_lo[:, :, :], tf_b[:, :, :], ct_hi[:, :, :], ct_l.sem)
                if h == 14 and has(st.prev, MLP):
                    pool.wait_ge(ln2_ve.sem, ln2_ve.after(st.prev))
                    g.tensor_tensor(rstd2[:, :], ve2[:, :], minus_half[:, :], ALU.pow).then_inc(ln2_rstd.sem, 1)
                if st.s is not None:
                    for u in UNIT_AT.get((st.s, h), ()):
                        pool.wait_ge(unit_hi, u + 1)
                        _, place, hi, lo = unit_io(u)
                        sub(lo, place, hi, unit_lo)

            steps(pool, lambda st: [slot(st, h) for h in range(H)])


def kernel(**inputs):
    import numpy as np
    import concourse.bacc as bacc
    from concourse.bass_utils import run_bass_kernel_spmd

    a = {k: np.asarray(v) for k, v in inputs.items()}
    l0 = {k[len("L0_xattn_"):]: v for k, v in a.items() if k.startswith("L0")}
    l1 = {k[len("L1_xattn_"):]: v for k, v in a.items() if k.startswith("L1")}
    none = np.zeros((D, D), np.float32)
    wa = np.stack([
        np.stack([l0[n].T for n in ("Wq", "Wk", "Wv", "Wo", "Wg")]),
        np.stack([l1["sa_" + n] for n in ("wq", "wk", "wv", "wo")] + [none]),
        np.stack([l1["ca_" + n] for n in ("wq", "wk", "wv", "wo")] + [none]),
    ])
    wm1 = np.stack([l0["W1"].T, l1["mlp_w1"]])
    wm2 = np.stack([l0["W2"].T, l1["mlp_w2"]])
    vectors = [l0["g1"], l0["be1"], l1["ln1_s"], l1["ln1_b"], l1["ln2_s"], l1["ln2_b"], l0["g2"], l0["be2"],
               l1["ln3_s"], l1["ln3_b"], l0["bq"], l0["bk"], l0["b1"], l1["mlp_b1"]]
    cols = np.concatenate([w.reshape(-1, P) for w in vectors]).T
    rows = np.stack([l0["bv"], l0["bo"], l0["bg"], l0["b2"], l1["mlp_b2"]])
    arrays = {"x": a["x"], "ctx": a["ctx_1024"], "mask": a["mask_BxSxS2_fk0"], "wa": wa, "wm1": wm1, "wm2": wm2,
              "cols": cols, "rows": rows, "ident": np.eye(P, dtype=np.float32)}
    arrays = {k: np.ascontiguousarray(v) for k, v in arrays.items()}

    nc = bacc.Bacc("TRN2", target_bir_lowering=False, num_devices=1)
    args = [nc.dram_tensor(k, v.shape, mybir.dt.from_np(v.dtype), kind="ExternalInput").ap() for k, v in arrays.items()]
    out = nc.dram_tensor("out", (B, S, D), F32, kind="ExternalOutput").ap()
    two_layers(nc, *args, out)
    r = run_bass_kernel_spmd(nc, [arrays], core_ids=[0])
    return r.results[0]["out"]
```

```python
from contextlib import ExitStack

import concourse.bass as bass
from concourse import mybir

F32 = mybir.dt.float32
F32R = mybir.dt.float32r
BF16 = mybir.dt.bfloat16
ALU = mybir.AluOpType
ACT = mybir.ActivationFunctionType
AX_X = mybir.AxisListType.X

P = 128
B, S, D = 16, 256, 256
H, HD = 16, 16
FF = 1024
KC = D // P
TT = S // P
FT = FF // P
CH = 4
NPASS = 3
MLP = (0, 2)
ALL = (0, 1, 2)
NTASK = NPASS * B
Q_PARTS = (0, 0, 1, 1, 0, 2)
K_PARTS = (0, 1, 0, 1, 2, 0)
NBLK = len(Q_PARTS)
ROWS = NBLK * HD
VW = HD + 1
LN_EPS = (1e-5, 1e-6, 1e-6)
MASKED = 1e9
HUGE = 3e38
WQ, WK, WV, WO, WG = range(5)
C_LN, C_LN2, C_BQ, C_BK, C_B1, NCOL = 0, 12, 20, 22, 24, 40
R_BV, R_BO, R_BG, R_B2, NROW = 0, 1, 2, 3, 5
UNITS = (("a", 0, (WQ, WK, WV)), ("a", 0, (WO, WG)), ("w1", 0, ()), ("w2", 0, ()),
         ("a", 1, (WQ, WK, WV)), ("a", 1, (WO,)), ("w1", 1, ()), ("w2", 1, ()),
         ("a", 2, (WQ, WK, WV)), ("a", 2, (WO,)))
LAG = 3
PV_LAG = 8
UNIT_AT = {(-2, 14): (0,), (-1, 13): (1,), (0, 3): (2,), (0, 12): (3,),
           (14, 9): (4,), (16, 13): (5,), (17, 9): (6,), (17, 14): (7,), (30, 9): (8,), (32, 13): (9,)}
UNIT_LOAD_AT = {(-2, 2): 0, (-1, 0): 1, (-1, 14): 2, (0, 5): 3, (1, 0): 4, (15, 0): 5, (17, 1): 6, (17, 11): 7,
                (18 - 1, 15): 8, (31, 0): 9}
UNIT_QKV, UNIT_O = {0: 0, 1: 4, 2: 8}, {0: 1, 1: 5, 2: 9}
GATE_AT, W2_AT = 10, (11, 12, 14)
O_AT = (13, 14, 13)
UNIT_W1, UNIT_W2 = {0: 2, 2: 6}, {0: 3, 2: 7}


class Task:

    def __init__(self, p, c, i=None):
        self.p, self.c, self.i, self.par = p, c, i, c % 2
        self.b = c if i is None else i * 2 + c
        self.first = i is None and c == 0


class Step:

    def __init__(self, s=None, p=0, j=0, i=None):
        self.s = s

        def at(off):
            if i is not None:
                return Task(p, 2 + j + off, i)
            return Task((s + off) // B, (s + off) % B) if 0 <= s + off < NTASK else None

        self.nxt2, self.nxt, self.cur = at(2), at(1), at(0)
        self.prev, self.old, self.older = at(-1), at(-2), at(-3)


def steps(eng, body):
    for s in range(-2, 2):
        body(Step(s))
    for p in range(NPASS):
        with eng.Fori(0, (B - 4) // 2) as i:
            for j in range(2):
                body(Step(p=p, j=j, i=i))
        for s in range(B * p + B - 2, B * p + B + 2):
            body(Step(s))


class Event:

    def __init__(self, sem, per=1, passes=ALL, credit=0):
        self.sem, self.per, self.passes, self.credit = sem, per, passes, credit

    def after(self, task, k=None):
        before = B * sum(q < task.p for q in self.passes)
        if task.p not in self.passes:
            return before * self.per + self.credit
        k = self.per if k is None else k
        const = (before + task.c) * self.per + k + self.credit
        return const if task.i is None else task.i * (2 * self.per) + const


class DmaEvent:

    def __init__(self, sems, dmas=1, passes=ALL, credit=0):
        self.sems, self.dmas, self.passes, self.credit = sems, dmas, passes, credit

    def of(self, task):
        return self.sems[task.par]

    def after(self, task):
        before = B * sum(q < task.p for q in self.passes)
        const = 16 * (self.dmas * ((before + task.c) // 2 + 1) + self.credit)
        return const if task.i is None else task.i * (16 * self.dmas) + const


def two_layers(nc, x, ctx, mask, wa, wm1, wm2, cols, rows, ident, out):
    with ExitStack() as es:
        def sb(name, shape, dt=F32):
            return es.enter_context(nc.sbuf_tensor(name, shape, dt))

        def sem(name):
            return es.enter_context(nc.semaphore(name))

        def ev(name, per=1, passes=ALL, credit=0):
            return Event(sem(name), per, passes, credit)

        def dev(name, dmas=1, passes=ALL, credit=0):
            return DmaEvent([sem(f"{name}_{i}") for i in range(2)], dmas, passes, credit)

        w_hi, w_lo = sb("w_hi", [P, 5, KC, D], F32R), sb("w_lo", [P, 5, KC, D], F32R)
        w1_hi, w1_lo = sb("w1_hi", [P, KC, FF], F32R), sb("w1_lo", [P, KC, FF], F32R)
        w2_hi, w2_lo = sb("w2_hi", [P, FT, D], F32R), sb("w2_lo", [P, FT, D], F32R)
        stage = sb("stage", [P, KC * FF])
        ident_sb = sb("ident_sb", [P, P])
        cols_sb = sb("cols_sb", [P, NCOL])
        rows_sb = sb("rows_sb", [P, NROW, D])
        minus_half = sb("minus_half", [P, TT])
        x_in = sb("x_in", [P, 2, TT, D])
        stats, mv, rstd = sb("stats", [P, TT, 6]), sb("mv", [P, TT, 2]), sb("rstd", [P, TT])
        stats2, mv2, rstd2 = sb("stats2", [P, TT, 6]), sb("mv2", [P, TT, 2]), sb("rstd2", [P, TT])
        ve, ve2 = sb("ve", [P, TT]), sb("ve2", [P, TT])
        tf_a, tf_b = sb("tf_a", [P, KC, S]), sb("tf_b", [P, KC, S])
        xt_hi, xt_lo = sb("xt_hi", [P, KC, S], F32R), sb("xt_lo", [P, KC, S], F32R)
        c_in = sb("c_in", [P, TT, D])
        ct_hi, ct_lo = sb("ct_hi", [P, KC, S], F32R), sb("ct_lo", [P, KC, S], F32R)
        q_f, k_f = sb("q_f", [P, KC, S]), sb("k_f", [P, KC, S])
        q_part, k_part = sb("q_part", [P, 3, KC, S], BF16), sb("k_part", [P, 3, KC, S], BF16)
        q_stack, k_stack = sb("q_stack", [ROWS, 2, H, S], BF16), sb("k_stack", [ROWS, 2, H, S], BF16)
        v_sb = sb("v_sb", [P, 2, TT, H, VW])
        prob = sb("prob", [P, 4, TT, S])
        neg_max = sb("neg_max", [P, 4, TT])
        prob_t = sb("prob_t", [P, 8, TT * S])
        o_t = sb("o_t", [P, CH, S])
        rden = sb("rden", [P, TT, H])
        o_sb = sb("o_sb", [P, TT, D])
        ot_hi, ot_lo = sb("ot_hi", [P, KC, S], F32R), sb("ot_lo", [P, KC, S], F32R)
        x_res = sb("x_res", [P, TT, D])
        x2 = sb("x2", [P, 2, TT, D])
        x2_hat = sb("x2_hat", [P, TT, D])
        x2t_hi, x2t_lo = sb("x2t_hi", [P, KC, S], F32R), sb("x2t_lo", [P, KC, S], F32R)
        h_f = sb("h_f", [P, 2, 2, S])
        h_hi, h_lo = sb("h_hi", [P, FT, S], F32R), sb("h_lo", [P, FT, S], F32R)
        y_sb = sb("y_sb", [P, TT, D])
        bias_sb = sb("bias_sb", [P, 2, TT, S])
        causal = sb("causal", [P, TT, S])

        s_ps = es.enter_context(nc.psum_tensor("s_ps", [P, 2, 512], F32))
        t_ps = es.enter_context(nc.psum_tensor("t_ps", [P, 2, 512], F32))
        o_ps = es.enter_context(nc.psum_tensor("o_ps", [P, 512], F32))
        m_ps = es.enter_context(nc.psum_tensor("m_ps", [P, 512], F32))
        d_ps = es.enter_context(nc.psum_tensor("d_ps", [P, 2, 512], F32))

        x_mid = nc.dram_tensor("x_mid", (2, B, S, D), F32, kind="Internal").ap()
        parts = nc.dram_tensor("parts", (2, 2, 3, H, HD, S), BF16, kind="Internal").ap()

        def tokens(dram):
            return dram.rearrange("(t p) d -> p t d", p=P)

        passed = sem("passed")
        const_landed, unit_landed = sem("const_landed"), sem("unit_landed")
        x_landed, res_landed = dev("x_landed"), dev("res_landed")
        ctx_landed, mask_landed = dev("ctx_landed", 1, MLP), dev("mask_landed", 1, (0,))
        q_written, k_written = dev("q_written", KC), dev("k_written", KC)
        stacked, stored = dev("stacked", 2 * NBLK), dev("stored", credit=1)
        xt_mm, ct_mm, x2t_mm = ev("xt_mm"), ev("ct_mm", 1, MLP), ev("x2t_mm", 1, MLP)
        q_mm, k_mm, v_mm = ev("q_mm"), ev("k_mm"), ev("v_mm")
        s_mm, t_mm, pv_mm = ev("s_mm", H), ev("t_mm", H), ev("pv_mm", CH)
        ot_mm, o2t_mm, proj_mm = ev("ot_mm", TT), ev("o2t_mm"), ev("proj_mm")
        w1_mm, w2_mm = ev("w1_mm", 4, MLP), ev("w2_mm", 1, MLP)
        xt_f, ct_f, x2t_f, ot_f = ev("xt_f"), ev("ct_f", 1, MLP), ev("x2t_f", 1, MLP), ev("ot_f")
        q_done, k_done = ev("q_done"), ev("k_done")
        p_done, pt_even, o_done = ev("p_done", H), ev("pt_even", H // 2), ev("o_done", CH)
        h_done = ev("h_done", 4, MLP)
        setup = sem("setup")
        causal_made, unit_hi, unit_lo = sem("causal_made"), sem("unit_hi"), sem("unit_lo")
        ln_stats, ln_mv, ln_ve, x_hat = ev("ln_stats"), ev("ln_mv"), ev("ln_ve"), ev("x_hat")
        ln2_stats, ln2_mv = ev("ln2_stats", 1, MLP), ev("ln2_mv", 1, MLP)
        ln2_ve, x2_hat_done = ev("ln2_ve", 1, MLP), ev("x2_hat_done", 1, MLP)
        xt_h, ct_h, x2t_h, ot_h = ev("xt_h"), ev("ct_h", 1, MLP), ev("x2t_h", 1, MLP), ev("ot_h")
        q_p1, q_p2, k_p1, k_p2 = ev("q_p1"), ev("q_p2"), ev("k_p1"), ev("k_p2")
        v_done, u_done, pt_odd = ev("v_done"), ev("u_done", H), ev("pt_odd", H // 2)
        bias_done, rden_done, o_norm = ev("bias_done", 1, (0,)), ev("rden_done", TT), ev("o_norm", TT)
        x2_done, h_h, y_done = ev("x2_done"), ev("h_h", 4, MLP), ev("y_done", 1, MLP, credit=1)
        ln_rstd, ln2_rstd = ev("ln_rstd"), ev("ln2_rstd", 1, MLP)
        xt_l, ct_l, x2t_l, ot_l = ev("xt_l"), ev("ct_l", 1, MLP), ev("x2t_l", 1, MLP), ev("ot_l")
        q_r, q_p3, k_r, k_p3 = ev("q_r"), ev("q_p3"), ev("k_r"), ev("k_p3")
        res_done, x2b_done, h_l = ev("res_done", 1, (0,)), ev("x2b_done", 1, MLP), ev("h_l", 4, MLP)

        def has(task, passes=ALL):
            return task is not None and task.p in passes

        def earlier_head(st, h, back):
            return (st.cur, h - back) if h >= back else (st.prev, h - back + H)

        def chunk_at(st, h, lag):
            return (st.cur, (h - lag) // CH) if h >= lag else (st.prev, (h - lag + H) // CH)

        def unit_io(u):
            kind, p, which = UNITS[u]
            if kind == "a":
                a, n = which[0], len(which)
                dram = wa[p, a:a + n].rearrange("w (k p) n -> p (w k) n", p=P)
                st = stage[:, 0:n * KC * D].rearrange("p (w n) -> p w n", n=D)
                return dram, st, *(w[:, a:a + n].rearrange("p w k n -> p (w k) n") for w in (w_hi, w_lo))
            if kind == "w1":
                st = stage[:, :].rearrange("p (k n) -> p k n", k=KC)
                return wm1[p].rearrange("(k p) n -> p k n", p=P), st, w1_hi[:, :, :], w1_lo[:, :, :]
            st = stage[:, :].rearrange("p (k n) -> p k n", k=FT)
            return wm2[p].rearrange("(k p) n -> p k n", p=P), st, w2_hi[:, :, :], w2_lo[:, :, :]

        def unit_users_done(eng, u):
            if u in (4, 8):
                eng.wait_ge(v_mm.sem, v_mm.after(Task(u // 4 - 1, B - 1)))
            if u in (5, 9):
                eng.wait_ge(proj_mm.sem, proj_mm.after(Task(u // 4 - 1, B - 1)))
            if u == 6:
                eng.wait_ge(w1_mm.sem, w1_mm.after(Task(0, B - 1)))
            if u == 7:
                eng.wait_ge(w2_mm.sem, w2_mm.after(Task(0, B - 1)))

        block = es.enter_context(nc.Block())

        @block.sync
        def _(sp):
            sp.dma_start(ident_sb[:, :], ident).then_inc(const_landed, 16)
            sp.dma_start(cols_sb[:, :], cols).then_inc(const_landed, 16)
            sp.dma_start(rows_sb[:, :, :], rows.partition_broadcast(P)).then_inc(const_landed, 16)

            for par in range(2):
                sp.sem_inc(stored.sems[par], 16)

            def source(task):
                return x[task.b] if task.p == 0 else x_mid[task.p - 1, task.b]

            def slot(st, h):
                if st.s is not None and (st.s, h) in UNIT_LOAD_AT:
                    u = UNIT_LOAD_AT[st.s, h]
                    if u:
                        sp.wait_ge(unit_hi, u)
                        sp.wait_ge(unit_lo, u)
                    dram, place, _, _ = unit_io(u)
                    sp.dma_start(place, dram).then_inc(unit_landed, 16)
                if h == 0 and has(st.nxt2, (2,)):
                    sp.wait_ge(ct_mm.sem, ct_mm.after(st.nxt if has(st.nxt, (2,)) else Task(0, B - 1)))
                    sp.sem_inc(passed, 1)
                    sp.dma_start(c_in[:, :, :], tokens(ctx[st.nxt2.b])).then_inc(ctx_landed.of(st.nxt2), 16)
                if h == 0 and has(st.nxt, (0,)):
                    if st.prev:
                        sp.wait_ge(u_done.sem, u_done.after(st.prev))
                        sp.sem_inc(passed, 1)
                    sp.dma_start(bias_sb[:, st.nxt.par], tokens(mask[st.nxt.b])).then_inc(mask_landed.of(st.nxt), 16)
                if h == 1 and has(st.nxt2):
                    if st.nxt2.p:
                        writer = Task(st.nxt2.p - 1, st.nxt2.c, st.nxt2.i)
                        sp.wait_ge(stored.of(writer), stored.after(writer))
                        sp.sem_inc(passed, 1)
                    if has(st.cur):
                        sp.wait_ge(xt_mm.sem, xt_mm.after(st.cur))
                        sp.sem_inc(passed, 1)
                    sp.dma_start(x_in[:, st.nxt2.par], tokens(source(st.nxt2))).then_inc(x_landed.of(st.nxt2), 16)
                if h == 2 and has(st.prev):
                    if st.old:
                        sp.wait_ge(x2_done.sem, x2_done.after(st.old))
                        sp.sem_inc(passed, 1)
                    sp.dma_start(x_res[:, :, :], tokens(source(st.prev))).then_inc(res_landed.of(st.prev), 16)
                if h == 6 and has(st.nxt):
                    t = st.nxt
                    if st.prev:
                        sp.wait_ge(stacked.of(st.prev), stacked.after(st.prev))
                        sp.sem_inc(passed, 1)
                    sp.wait_ge(q_p2.sem, q_p2.after(t))
                    sp.sem_inc(passed, 1)
                    sp.wait_ge(q_p3.sem, q_p3.after(t))
                    sp.sem_inc(passed, 1)
                    for m in range(KC):
                        sp.dma_start(parts[t.par, 0, :, m * 8:m * 8 + 8].rearrange("j h d s -> (h d) j s"),
                                     q_part[:, :, m, :]).then_inc(q_written.of(t), 16)
                if h == 7 and has(st.nxt):
                    t = st.nxt
                    sp.wait_ge(k_p2.sem, k_p2.after(t))
                    sp.sem_inc(passed, 1)
                    sp.wait_ge(k_p3.sem, k_p3.after(t))
                    sp.sem_inc(passed, 1)
                    for m in range(KC):
                        sp.dma_start(parts[t.par, 1, :, m * 8:m * 8 + 8].rearrange("j h d s -> (h d) j s"),
                                     k_part[:, :, m, :]).then_inc(k_written.of(t), 16)
                    if st.prev:
                        sp.wait_ge(s_mm.sem, s_mm.after(st.prev))
                        sp.sem_inc(passed, 1)
                    sp.wait_ge(q_written.of(t), q_written.after(t))
                    sp.sem_inc(passed, 1)
                    for j, part in enumerate(Q_PARTS):
                        sp.dma_start(q_stack[j * HD:(j + 1) * HD, t.par],
                                     parts[t.par, 0, part].rearrange("h d s -> d h s")).then_inc(stacked.of(t), 16)
                    sp.wait_ge(k_written.of(t), k_written.after(t))
                    sp.sem_inc(passed, 1)
                    for j, part in enumerate(K_PARTS):
                        sp.dma_start(k_stack[j * HD:(j + 1) * HD, t.par],
                                     parts[t.par, 1, part].rearrange("h d s -> d h s")).then_inc(stacked.of(t), 16)
                if h == 12 and has(st.cur, (0,)):
                    if st.prev:
                        sp.wait_ge(ct_mm.sem, ct_mm.after(st.prev))
                        sp.sem_inc(passed, 1)
                    sp.dma_start(c_in[:, :, :], tokens(ctx[st.cur.b])).then_inc(ctx_landed.of(st.cur), 16)
                if h == 15 and has(st.prev, (1,)):
                    sp.wait_ge(x2_done.sem, x2_done.after(st.prev))
                    sp.sem_inc(passed, 1)
                    sp.dma_start(tokens(x_mid[1, st.prev.b]), x2[:, st.prev.par]).then_inc(stored.of(st.prev), 16)
                if h == 15 and has(st.old, MLP):
                    sp.wait_ge(y_done.sem, y_done.after(st.old))
                    sp.sem_inc(passed, 1)
                    dst = x_mid[0, st.old.b] if st.old.p == 0 else out[st.old.b]
                    sp.dma_start(tokens(dst), y_sb[:, :, :]).then_inc(stored.of(st.old), 16)

            steps(sp, lambda st: [slot(st, h) for h in range(H)])
            for b in (B - 2, B - 1):
                sp.wait_ge(stored.of(Task(NPASS - 1, b)), stored.after(Task(NPASS - 1, b)))
                sp.sem_inc(passed, 1)

        @block.tensor
        def _(pe):
            mm = nc.tensor.matmul
            pe.wait_ge(const_landed, 48)
            pe.wait_ge(setup, 3)

            def product(dst, pairs, opens=True, closes=True):
                terms = [t for lh, ll, rh, rl in pairs for t in ((lh, rh), (lh, rl), (ll, rh))]
                for n, (lhs, rhs) in enumerate(terms):
                    last = mm(dst, lhs, rhs, start=(opens and n == 0), stop=(closes and n == len(terms) - 1))
                return last

            def flip(dst, src):
                for k in range(KC):
                    for t in range(TT):
                        last = nc.tensor.transpose(dst[:, k * S + t * P:k * S + (t + 1) * P],
                                                   src[:, t, k * P:(k + 1) * P], ident_sb[:, :])
                return last

            def features(bank, w, src_hi, src_lo):
                for m in range(KC):
                    c = slice(m * P, (m + 1) * P)
                    last = product(d_ps[:, bank, m * S:(m + 1) * S],
                                   [(w_hi[:, w, k, c], w_lo[:, w, k, c], src_hi[:, k, :], src_lo[:, k, :])
                                    for k in range(KC)])
                return last

            def bank_1_free(st):
                if has(st.old, MLP):
                    pe.wait_ge(h_done.sem, h_done.after(st.old))
                elif st.nxt:
                    pe.wait_ge(v_done.sem, v_done.after(st.nxt))
                else:
                    pe.wait_ge(x2_done.sem, x2_done.after(st.old))

            def by_token(bank, sources, opens=True, closes=True):
                for t in range(TT):
                    c = slice(t * P, (t + 1) * P)
                    last = product(d_ps[:, bank, t * D:(t + 1) * D],
                                   [(a_hi[:, k, c], a_lo[:, k, c], w_hi[:, w, k, :], w_lo[:, w, k, :])
                                    for a_hi, a_lo, w in sources for k in range(KC)],
                                   opens and t == 0, closes and t == TT - 1)
                return last

            def weights(task, units):
                if task.first:
                    pe.wait_ge(unit_hi, units[task.p] + 1)
                    pe.wait_ge(unit_lo, units[task.p] + 1)

            def scores(st, h):
                t = st.cur
                if h == 0:
                    pe.wait_ge(stacked.of(t), stacked.after(t))
                before, hb = earlier_head(st, h, 2)
                if has(before, (2,)):
                    pe.wait_ge(p_done.sem, p_done.after(before, hb + 1))
                elif before:
                    pe.wait_ge(u_done.sem, u_done.after(before, hb + 1))
                for q in range(TT):
                    n = (q + 1) * P if t.p == 1 else S
                    last = mm(s_ps[:, h % 2, q * S:q * S + n], q_stack[:, t.par, h, q * P:(q + 1) * P],
                              k_stack[:, t.par, h, 0:n], start=True, stop=True)
                last.then_inc(s_mm.sem, 1)

            def transposed_probs(t, h, st):
                pe.wait_ge(p_done.sem, p_done.after(t, h + 1))
                before, hb = (t, h - 2) if h >= 2 else (st.prev if t is st.cur else st.old, h + H - 2)
                if before and h % 2:
                    pe.wait_ge(pt_odd.sem, pt_odd.after(before, hb // 2 + 1))
                elif before:
                    pe.wait_ge(pt_even.sem, pt_even.after(before, hb // 2 + 1))
                for k in range(TT):
                    for q in range(TT):
                        if t.p == 1 and k > q:
                            continue
                        c = k * S + (q * P if not (t.p == 1 and k) else 0)
                        last = nc.tensor.transpose(t_ps[:, h % 2, c:c + P],
                                                   prob[:, h % 4, q, k * P:(k + 1) * P], ident_sb[:, :])
                last.then_inc(t_mm.sem, 1)

            def values(st, t, c):
                if c == 0:
                    pe.wait_ge(v_done.sem, v_done.after(t))
                    before = st.prev
                else:
                    before = t
                pe.wait_ge(pt_even.sem, pt_even.after(t, 2 * c + 2))
                pe.wait_ge(pt_odd.sem, pt_odd.after(t, 2 * c + 2))
                if before:
                    pe.wait_ge(o_done.sem, o_done.after(before, (c - 1) % CH + 1))
                for k in range(TT):
                    lo = P if (t.p == 1 and k) else 0
                    for j in range(CH):
                        h = CH * c + j
                        last = mm(o_ps[32 * j:32 * j + VW, lo:S], v_sb[:, t.par, k, h, :],
                                  prob_t[:, h % 8, k * S:k * S + S - lo], start=(k == 0), stop=(k == TT - 1),
                                  tile_position=(0, 32 * j))
                last.then_inc(pv_mm.sem, 1)

            def head_tokens(st, q):
                t = st.prev
                if q == 0:
                    pe.wait_ge(o_done.sem, o_done.after(t))
                    if has(t, (0,)):
                        pe.wait_ge(ct_f.sem, ct_f.after(t))
                    elif has(st.nxt2, (2,)):
                        pe.wait_ge(ct_f.sem, ct_f.after(st.nxt2))
                    elif has(st.old, MLP):
                        pe.wait_ge(x2t_f.sem, x2t_f.after(st.old))
                    elif st.nxt:
                        pe.wait_ge(xt_f.sem, xt_f.after(st.nxt))
                else:
                    pe.wait_ge(o_norm.sem, o_norm.after(t, 1))
                for c in range(CH):
                    last = nc.tensor.transpose(m_ps[:, c * P:(c + 1) * P], o_t[:, c, q * P:(q + 1) * P],
                                               ident_sb[:, :])
                last.then_inc(ot_mm.sem, 1)

            def slot(st, h):
                if has(st.cur):
                    scores(st, h)
                t, ht = earlier_head(st, h, LAG)
                if t is not None:
                    transposed_probs(t, ht, st)
                if h == 1 and has(st.old, MLP):
                    pe.wait_ge(x2_hat_done.sem, x2_hat_done.after(st.old))
                    if st.nxt:
                        pe.wait_ge(xt_f.sem, xt_f.after(st.nxt))
                    else:
                        pe.wait_ge(ot_f.sem, ot_f.after(st.old))
                    flip(m_ps, x2_hat).then_inc(x2t_mm.sem, 1)
                if h == 2 and has(st.nxt):
                    weights(st.nxt, UNIT_QKV)
                    pe.wait_ge(xt_h.sem, xt_h.after(st.nxt))
                    pe.wait_ge(xt_l.sem, xt_l.after(st.nxt))
                    if st.old:
                        pe.wait_ge(x2_done.sem, x2_done.after(st.old))
                    elif st.cur:
                        pe.wait_ge(v_done.sem, v_done.after(st.cur))
                    features(1, WQ, xt_hi, xt_lo).then_inc(q_mm.sem, 1)
                kv = (ct_hi, ct_lo) if has(st.nxt, (2,)) else (xt_hi, xt_lo)
                if h == 3 and has(st.nxt):
                    if has(st.nxt, (2,)):
                        pe.wait_ge(ct_h.sem, ct_h.after(st.nxt))
                        pe.wait_ge(ct_l.sem, ct_l.after(st.nxt))
                    if st.cur:
                        pe.wait_ge(k_done.sem, k_done.after(st.cur))
                    if st.older:
                        pe.wait_ge(y_done.sem, y_done.after(st.older))
                    features(0, WK, *kv).then_inc(k_mm.sem, 1)
                if h == 4 and has(st.nxt):
                    pe.wait_ge(q_done.sem, q_done.after(st.nxt))
                    by_token(1, [(*kv, WV)]).then_inc(v_mm.sem, 1)
                if h == 4 and has(st.prev, (0,)):
                    pe.wait_ge(ctx_landed.of(st.prev), ctx_landed.after(st.prev))
                    if st.old:
                        pe.wait_ge(x2t_f.sem, x2t_f.after(st.old))
                    else:
                        pe.wait_ge(xt_f.sem, xt_f.after(st.nxt))
                    flip(m_ps, c_in).then_inc(ct_mm.sem, 1)
                if h == 4 and has(st.nxt2, (2,)):
                    pe.wait_ge(ctx_landed.of(st.nxt2), ctx_landed.after(st.nxt2))
                    if has(st.old, MLP):
                        pe.wait_ge(x2t_f.sem, x2t_f.after(st.old))
                    else:
                        pe.wait_ge(xt_f.sem, xt_f.after(st.nxt))
                    flip(m_ps, c_in).then_inc(ct_mm.sem, 1)
                if 5 <= h <= 8 and has(st.old, MLP):
                    n = h - 5
                    if n == 0:
                        weights(st.old, UNIT_W1)
                        pe.wait_ge(x2t_h.sem, x2t_h.after(st.old))
                        pe.wait_ge(x2t_l.sem, x2t_l.after(st.old))
                        if st.nxt:
                            pe.wait_ge(k_done.sem, k_done.after(st.nxt))
                        else:
                            pe.wait_ge(y_done.sem, y_done.after(st.older))
                    elif n == 1:
                        if st.nxt:
                            pe.wait_ge(v_done.sem, v_done.after(st.nxt))
                        else:
                            pe.wait_ge(x2_done.sem, x2_done.after(st.old))
                    else:
                        pe.wait_ge(h_done.sem, h_done.after(st.old, n - 1))
                    for f in range(2):
                        c = slice((2 * n + f) * P, (2 * n + f + 1) * P)
                        last = product(d_ps[:, n % 2, f * S:(f + 1) * S],
                                       [(w1_hi[:, k, c], w1_lo[:, k, c], x2t_hi[:, k, :], x2t_lo[:, k, :])
                                        for k in range(KC)])
                    last.then_inc(w1_mm.sem, 1)
                if h in (6, 8) and has(st.prev):
                    head_tokens(st, (h - 6) // 2)
                if h == 10 and has(st.prev):
                    pe.wait_ge(o_norm.sem, o_norm.after(st.prev))
                    flip(m_ps, o_sb).then_inc(o2t_mm.sem, 1)
                if h == GATE_AT and has(st.prev, (0,)):
                    weights(st.prev, UNIT_O)
                    pe.wait_ge(ct_h.sem, ct_h.after(st.prev))
                    pe.wait_ge(ct_l.sem, ct_l.after(st.prev))
                    bank_1_free(st)
                    by_token(1, [(ct_hi, ct_lo, WG)], closes=False)
                if has(st.prev) and h == O_AT[st.prev.p]:
                    t = st.prev
                    pe.wait_ge(ot_h.sem, ot_h.after(t))
                    pe.wait_ge(ot_l.sem, ot_l.after(t))
                    if t.p:
                        weights(t, UNIT_O)
                        bank_1_free(st)
                    by_token(1, [(ot_hi, ot_lo, WO)], opens=t.p > 0).then_inc(proj_mm.sem, 1)
                if h in W2_AT and has(st.old, MLP):
                    part = W2_AT.index(h)
                    if part == 0:
                        weights(st.old, UNIT_W2)
                        pe.wait_ge(h_done.sem, h_done.after(st.old, 3))
                    pe.wait_ge(h_l.sem, h_l.after(st.old, min(part + 3, 4)))
                    terms = [(t, f, n) for t in range(TT) for f in range(FT) for n in range(3)]
                    each = len(terms) // len(W2_AT)
                    for t, f, n in terms[part * each:(part + 1) * each]:
                        c = slice(t * P, (t + 1) * P)
                        lhs = (h_hi, h_hi, h_lo)[n][:, f, c]
                        rhs = (w2_hi, w2_lo, w2_hi)[n][:, f, :]
                        last = mm(d_ps[:, 0, t * D:(t + 1) * D], lhs, rhs, start=(f == 0 and n == 0),
                                  stop=(f == FT - 1 and n == 2))
                    if part == len(W2_AT) - 1:
                        last.then_inc(w2_mm.sem, 1)
                if h == 13 and has(st.nxt2):
                    pe.wait_ge(x_hat.sem, x_hat.after(st.nxt2))
                    if st.prev:
                        pe.wait_ge(ot_f.sem, ot_f.after(st.prev))
                    elif st.nxt:
                        pe.wait_ge(xt_f.sem, xt_f.after(st.nxt))
                    flip(m_ps, x_in[:, st.nxt2.par]).then_inc(xt_mm.sem, 1)
                if h % CH == 0:
                    t, c = chunk_at(st, h, PV_LAG)
                    if t is not None:
                        values(st, t, c)

            steps(pe, lambda st: [slot(st, h) for h in range(H)])

        @block.scalar
        def _(act):
            act.wait_ge(const_landed, 48)
            act.wait_ge(setup, 2)

            def probs(st, h):
                t = st.cur
                act.wait_ge(u_done.sem, u_done.after(t, h + 1))
                if t.p == 2:
                    before, hb = earlier_head(st, h, 4)
                    if before:
                        act.wait_ge(t_mm.sem, t_mm.after(before, hb + 1))
                for q in range(TT):
                    n = (q + 1) * P if t.p == 1 else S
                    src = s_ps[:, h % 2, q * S:q * S + n] if t.p == 2 else prob[:, h % 4, q, 0:n]
                    last = nc.scalar.activation(prob[:, h % 4, q, 0:n], src, ACT.Exp,
                                                bias=neg_max[:, h % 4, q:q + 1], scale=-1.0)
                last.then_inc(p_done.sem, 1)

            def affine(dst, col_g, col_b, done):
                for k in range(KC):
                    last = nc.scalar.activation(dst[:, k, :], m_ps[:, k * S:(k + 1) * S], ACT.Identity,
                                                bias=cols_sb[:, col_b + k:col_b + k + 1],
                                                scale=cols_sb[:, col_g + k:col_g + k + 1])
                last.then_inc(done.sem, 1)

            def slot(st, h):
                if h % CH == 1:
                    t, c = chunk_at(st, h, PV_LAG + 1)
                    if t is not None:
                        act.wait_ge(pv_mm.sem, pv_mm.after(t, c + 1))
                        if c == 0:
                            if st.prev:
                                act.wait_ge(ot_mm.sem, ot_mm.after(st.prev))
                        nc.scalar.activation(o_t[:, c, :], o_ps[:, 0:S], ACT.Copy).then_inc(o_done.sem, 1)
                if h == 2 and has(st.old, MLP):
                    act.wait_ge(x2t_mm.sem, x2t_mm.after(st.old))
                    if has(st.old, (0,)):
                        act.wait_ge(ct_h.sem, ct_h.after(st.old))
                        act.wait_ge(ct_l.sem, ct_l.after(st.old))
                    else:
                        if st.nxt:
                            act.wait_ge(ct_l.sem, ct_l.after(st.nxt))
                    c = C_LN2 + 4 * MLP.index(st.old.p)
                    affine(tf_b, c, c + 2, x2t_f)
                if h == 3 and has(st.nxt):
                    act.wait_ge(q_mm.sem, q_mm.after(st.nxt))
                    if st.cur:
                        act.wait_ge(q_p3.sem, q_p3.after(st.cur))
                    if st.nxt.p == 0:
                        for m in range(KC):
                            last = nc.scalar.activation(q_f[:, m, :], d_ps[:, 1, m * S:(m + 1) * S], ACT.Identity,
                                                        bias=cols_sb[:, C_BQ + m:C_BQ + m + 1], scale=-0.25)
                    else:
                        last = nc.scalar.activation(q_f[:, :, :], d_ps[:, 1, :].rearrange("p (m s) -> p m s", m=KC),
                                                    ACT.Copy, scale=-0.25)
                    last.then_inc(q_done.sem, 1)
                if h == 4 and has(st.nxt):
                    act.wait_ge(k_mm.sem, k_mm.after(st.nxt))
                    if st.cur:
                        act.wait_ge(k_p3.sem, k_p3.after(st.cur))
                    if st.nxt.p == 0:
                        for m in range(KC):
                            last = nc.scalar.activation(k_f[:, m, :], d_ps[:, 0, m * S:(m + 1) * S], ACT.Identity,
                                                        bias=cols_sb[:, C_BK + m:C_BK + m + 1])
                    else:
                        last = nc.scalar.activation(k_f[:, :, :], d_ps[:, 0, :].rearrange("p (m s) -> p m s", m=KC),
                                                    ACT.Copy)
                    last.then_inc(k_done.sem, 1)
                if h == 5 and has(st.prev, (0,)):
                    act.wait_ge(ct_mm.sem, ct_mm.after(st.prev))
                    if st.old:
                        act.wait_ge(x2t_h.sem, x2t_h.after(st.old))
                        act.wait_ge(x2t_l.sem, x2t_l.after(st.old))
                        act.wait_ge(ct_l.sem, ct_l.after(st.old))
                    nc.scalar.activation(tf_b[:, :, :], m_ps[:, :].rearrange("p (k s) -> p k s", k=KC), ACT.Copy)\
                        .then_inc(ct_f.sem, 1)
                if 6 <= h <= 9 and has(st.old, MLP):
                    n = h - 6
                    act.wait_ge(w1_mm.sem, w1_mm.after(st.old, n + 1))
                    if n >= 2:
                        act.wait_ge(h_h.sem, h_h.after(st.old, n - 1))
                        act.wait_ge(h_l.sem, h_l.after(st.old, n - 1))
                    for f in range(2):
                        c = C_B1 + FT * MLP.index(st.old.p) + 2 * n + f
                        last = nc.scalar.activation(h_f[:, n % 2, f, :], d_ps[:, n % 2, f * S:(f + 1) * S], ACT.Relu,
                                                    bias=cols_sb[:, c:c + 1])
                    last.then_inc(h_done.sem, 1)
                if h == 11 and has(st.prev):
                    act.wait_ge(o2t_mm.sem, o2t_mm.after(st.prev))
                    if st.nxt:
                        act.wait_ge(xt_l.sem, xt_l.after(st.nxt))
                    else:
                        act.wait_ge(ot_l.sem, ot_l.after(st.old))
                    nc.scalar.activation(tf_a[:, :, :], m_ps[:, :].rearrange("p (k s) -> p k s", k=KC), ACT.Copy)\
                        .then_inc(ot_f.sem, 1)
                if h == 5 and has(st.nxt2, (2,)):
                    act.wait_ge(ct_mm.sem, ct_mm.after(st.nxt2))
                    if has(st.old, MLP):
                        act.wait_ge(x2t_l.sem, x2t_l.after(st.old))
                    else:
                        act.wait_ge(ct_l.sem, ct_l.after(st.nxt))
                    nc.scalar.activation(tf_b[:, :, :], m_ps[:, :].rearrange("p (k s) -> p k s", k=KC), ACT.Copy)\
                        .then_inc(ct_f.sem, 1)
                if h == 14 and has(st.nxt2):
                    act.wait_ge(xt_mm.sem, xt_mm.after(st.nxt2))
                    if st.prev:
                        act.wait_ge(ot_l.sem, ot_l.after(st.prev))
                    elif st.nxt:
                        act.wait_ge(xt_l.sem, xt_l.after(st.nxt))
                    c = C_LN + 4 * st.nxt2.p
                    affine(tf_a, c, c + 2, xt_f)
                t, ht = earlier_head(st, h, LAG)
                if t is not None and ht % 2 == 0:
                    act.wait_ge(t_mm.sem, t_mm.after(t, ht + 1))
                    back = (t, ht - 8) if ht >= 8 else (st.prev if t is st.cur else st.old, ht + 8)
                    if back[0] and ht % CH < 2:
                        act.wait_ge(pv_mm.sem, pv_mm.after(back[0], back[1] // CH + 1))
                    n = 384 if t.p == 1 else 512
                    nc.scalar.activation(prob_t[:, ht % 8, 0:n], t_ps[:, 0, 0:n], ACT.Copy).then_inc(pt_even.sem, 1)
                if has(st.cur):
                    probs(st, h)

            steps(act, lambda st: [slot(st, h) for h in range(H)])

        @block.vector
        def _(dve):
            v = nc.vector
            v.memset(o_ps[:, :], 0.0).then_inc(setup, 1)
            dve.wait_ge(const_landed, 48)
            v.tensor_scalar(cols_sb[:, C_BQ:C_BQ + KC], cols_sb[:, C_BQ:C_BQ + KC], -0.25, None, ALU.mult)\
                .then_inc(setup, 1)
            v.memset(v_sb[:, :, :, :, HD:VW], 1.0).then_inc(setup, 1)

            def score_guard(st, h):
                t = st.cur
                dve.wait_ge(s_mm.sem, s_mm.after(t, h + 1))
                before, hb = earlier_head(st, h, 4)
                if t.p == 2:
                    if before:
                        dve.wait_ge(p_done.sem, p_done.after(before, hb + 1))
                    v.tensor_reduce(neg_max[:, h % 4, :], s_ps[:, h % 2, :].rearrange("p (q k) -> p q k", q=TT),
                                    AX_X, ALU.min).then_inc(u_done.sem, 1)
                    return
                if before:
                    dve.wait_ge(t_mm.sem, t_mm.after(before, hb + 1))
                if h == 0 and t.p == 0:
                    dve.wait_ge(bias_done.sem, bias_done.after(t))
                if h == 0 and t.first and t.p == 1:
                    dve.wait_ge(causal_made, 3)
                dve.sem_inc(passed, 1)
                for q in range(TT):
                    n = (q + 1) * P if t.p == 1 else S
                    bias = causal[:, q, 0:n] if t.p == 1 else bias_sb[:, t.par, q, 0:n]
                    last = v.tensor_tensor_reduce(prob[:, h % 4, q, 0:n], s_ps[:, h % 2, q * S:q * S + n], bias,
                                                  1.0, HUGE, ALU.add, ALU.min, neg_max[:, h % 4, q:q + 1])
                last.then_inc(u_done.sem, 1)

            def statistics(src, st_t, done):
                for t in range(TT):
                    last = v.bn_stats(st_t[:, t, :], src[:, t, :])
                last.then_inc(done.sem, 1)

            def aggregate(task, st_t, mv_t, ve_t, eps, stats_done, mv_done, ve_done):
                dve.wait_ge(stats_done.sem, stats_done.after(task))
                dve.sem_inc(passed, 1)
                for t in range(TT):
                    last = v.bn_aggr(mv_t[:, t, :], st_t[:, t, :])
                last.then_inc(mv_done.sem, 1)
                dve.wait_ge(mv_done.sem, mv_done.after(task))
                v.tensor_scalar(ve_t[:, :], mv_t[:, :, 1], eps, None, ALU.add).then_inc(ve_done.sem, 1)

            def normalise(dst, src, mv_t, rstd_t, done):
                for t in range(TT):
                    last = v.tensor_scalar(dst[:, t, :], src[:, t, :], mv_t[:, t, 0:1], rstd_t[:, t:t + 1],
                                           ALU.subtract, ALU.mult)
                last.then_inc(done.sem, 1)

            def slot(st, h):
                if h in (7, 9) and has(st.prev):
                    q = (h - 7) // 2
                    dve.wait_ge(ot_mm.sem, ot_mm.after(st.prev, q + 1))
                    if st.old:
                        dve.wait_ge(o2t_mm.sem, o2t_mm.after(st.old))
                    o = m_ps[:, :].rearrange("p (h w) -> p h w", w=32)
                    v.reciprocal(rden[:, q, :], o[:, :, HD]).then_inc(rden_done.sem, 1)
                    dve.wait_ge(rden_done.sem, rden_done.after(st.prev, q + 1))
                    v.tensor_tensor(o_sb[:, q, :].rearrange("p (h d) -> p h d", d=HD), o[:, :, 0:HD],
                                    rden[:, q, :].unsqueeze(2).to_broadcast([P, H, HD]), ALU.mult)\
                        .then_inc(o_norm.sem, 1)
                if h == 3 and has(st.old, MLP):
                    dve.wait_ge(x2t_f.sem, x2t_f.after(st.old))
                    v.tensor_copy(x2t_hi[:, :, :], tf_b[:, :, :]).then_inc(x2t_h.sem, 1)
                if h == 3 and has(st.nxt, (0,)):
                    dve.wait_ge(mask_landed.of(st.nxt), mask_landed.after(st.nxt))
                    v.tensor_scalar(bias_sb[:, st.nxt.par], bias_sb[:, st.nxt.par], 1.0, -MASKED,
                                    ALU.subtract, ALU.mult).then_inc(bias_done.sem, 1)
                if h == 4 and has(st.nxt):
                    dve.wait_ge(q_done.sem, q_done.after(st.nxt))
                    if st.cur:
                        dve.wait_ge(q_written.of(st.cur), q_written.after(st.cur))
                    v.tensor_copy(q_part[:, 0], q_f[:, :, :]).then_inc(q_p1.sem, 1)
                if h == 5 and has(st.nxt):
                    dve.wait_ge(k_done.sem, k_done.after(st.nxt))
                    if st.cur:
                        dve.wait_ge(k_written.of(st.cur), k_written.after(st.cur))
                    v.tensor_copy(k_part[:, 0], k_f[:, :, :]).then_inc(k_p1.sem, 1)
                    dve.wait_ge(q_r.sem, q_r.after(st.nxt))
                    v.tensor_copy(q_part[:, 1], q_f[:, :, :]).then_inc(q_p2.sem, 1)
                    dve.wait_ge(v_mm.sem, v_mm.after(st.nxt))
                    if st.prev:
                        dve.wait_ge(pv_mm.sem, pv_mm.after(st.prev))
                    for k in range(TT):
                        dst = v_sb[:, st.nxt.par, k, :, 0:HD]
                        src = d_ps[:, 1, k * D:(k + 1) * D].rearrange("p (h d) -> p h d", d=HD)
                        if st.nxt.p == 0:
                            bv = rows_sb[:, R_BV, :].rearrange("p (h d) -> p h d", d=HD)
                            last = v.tensor_tensor(dst, src, bv, ALU.add)
                        else:
                            last = v.tensor_copy(dst, src)
                    last.then_inc(v_done.sem, 1)
                if h == 6 and has(st.nxt):
                    dve.wait_ge(k_r.sem, k_r.after(st.nxt))
                    v.tensor_copy(k_part[:, 1], k_f[:, :, :]).then_inc(k_p2.sem, 1)
                if h == 6 and has(st.prev, (0,)):
                    dve.wait_ge(ct_f.sem, ct_f.after(st.prev))
                    if st.old:
                        dve.wait_ge(proj_mm.sem, proj_mm.after(st.old))
                    v.tensor_copy(ct_hi[:, :, :], tf_b[:, :, :]).then_inc(ct_h.sem, 1)
                if 7 <= h <= 10 and has(st.old, MLP):
                    n = h - 7
                    dve.wait_ge(h_done.sem, h_done.after(st.old, n + 1))
                    v.tensor_copy(h_hi[:, 2 * n:2 * n + 2, :], h_f[:, n % 2]).then_inc(h_h.sem, 1)
                if h == 12 and has(st.prev):
                    dve.wait_ge(ot_f.sem, ot_f.after(st.prev))
                    if st.old:
                        dve.wait_ge(proj_mm.sem, proj_mm.after(st.old))
                    v.tensor_copy(ot_hi[:, :, :], tf_a[:, :, :]).then_inc(ot_h.sem, 1)
                if h == 9 and has(st.nxt2):
                    dve.wait_ge(x_landed.of(st.nxt2), x_landed.after(st.nxt2))
                    if st.nxt:
                        dve.wait_ge(ln_mv.sem, ln_mv.after(st.nxt))
                    statistics(x_in[:, st.nxt2.par], stats, ln_stats)
                if h == 10 and has(st.nxt2):
                    if st.nxt:
                        dve.wait_ge(x_hat.sem, x_hat.after(st.nxt))
                        dve.wait_ge(ln_rstd.sem, ln_rstd.after(st.nxt))
                    aggregate(st.nxt2, stats, mv, ve, LN_EPS[st.nxt2.p], ln_stats, ln_mv, ln_ve)
                if h == 12 and has(st.nxt2):
                    dve.wait_ge(ln_rstd.sem, ln_rstd.after(st.nxt2))
                    normalise(x_in[:, st.nxt2.par], x_in[:, st.nxt2.par], mv, rstd, x_hat)
                if h == 6 and has(st.nxt2, (2,)):
                    dve.wait_ge(ct_f.sem, ct_f.after(st.nxt2))
                    if st.nxt:
                        dve.wait_ge(v_mm.sem, v_mm.after(st.nxt))
                    v.tensor_copy(ct_hi[:, :, :], tf_b[:, :, :]).then_inc(ct_h.sem, 1)
                if has(st.prev) and h == O_AT[st.prev.p] + 1:
                    t = st.prev
                    dve.wait_ge(proj_mm.sem, proj_mm.after(t))
                    if t.p == 0:
                        dve.wait_ge(res_done.sem, res_done.after(t))
                    else:
                        dve.wait_ge(res_landed.of(t), res_landed.after(t))
                    if st.older:
                        dve.wait_ge(stored.of(st.older), stored.after(st.older))
                    v.tensor_tensor(x2[:, t.par], d_ps[:, 1, :].rearrange("p (t d) -> p t d", t=TT),
                                    x_res[:, :, :], ALU.add).then_inc(x2_done.sem, 1)
                if h == 14 and has(st.prev, MLP):
                    t = st.prev
                    dve.wait_ge(x2_done.sem, x2_done.after(t))
                    if st.old:
                        dve.wait_ge(ln2_mv.sem, ln2_mv.after(st.old))
                    statistics(x2[:, t.par], stats2, ln2_stats)
                    if st.old:
                        dve.wait_ge(x2_hat_done.sem, x2_hat_done.after(st.old))
                        dve.wait_ge(ln2_rstd.sem, ln2_rstd.after(st.old))
                    aggregate(t, stats2, mv2, ve2, LN_EPS[t.p], ln2_stats, ln2_mv, ln2_ve)
                if h == 15 and has(st.prev, MLP):
                    dve.wait_ge(ln2_rstd.sem, ln2_rstd.after(st.prev))
                    if st.old:
                        dve.wait_ge(x2t_mm.sem, x2t_mm.after(st.old))
                    normalise(x2_hat, x2[:, st.prev.par], mv2, rstd2, x2_hat_done)
                if h == 15 and has(st.old, MLP):
                    dve.wait_ge(w2_mm.sem, w2_mm.after(st.old))
                    dve.wait_ge(x2b_done.sem, x2b_done.after(st.old))
                    if st.older:
                        dve.wait_ge(stored.of(st.older), stored.after(st.older))
                    v.tensor_tensor(y_sb[:, :, :], d_ps[:, 0, :].rearrange("p (t d) -> p t d", t=TT),
                                    x2[:, st.old.par], ALU.add).then_inc(y_done.sem, 1)
                if has(st.cur):
                    score_guard(st, h)
                t, ht = earlier_head(st, h, LAG)
                if t is not None and ht % 2:
                    dve.wait_ge(t_mm.sem, t_mm.after(t, ht + 1))
                    back = (t, ht - 8) if ht >= 8 else (st.prev if t is st.cur else st.old, ht + 8)
                    if back[0] and ht % CH < 2:
                        dve.wait_ge(pv_mm.sem, pv_mm.after(back[0], back[1] // CH + 1))
                    n = 384 if t.p == 1 else 512
                    v.tensor_copy(prob_t[:, ht % 8, 0:n], t_ps[:, 1, 0:n]).then_inc(pt_odd.sem, 1)
                if h == 15 and has(st.nxt2):
                    dve.wait_ge(xt_f.sem, xt_f.after(st.nxt2))
                    if st.nxt:
                        dve.wait_ge(v_mm.sem, v_mm.after(st.nxt))
                    v.tensor_copy(xt_hi[:, :, :], tf_a[:, :, :]).then_inc(xt_h.sem, 1)
                if st.s is not None:
                    for u in UNIT_AT.get((st.s, h), ()):
                        dve.wait_ge(unit_landed, 16 * (u + 1))
                        unit_users_done(dve, u)
                        _, place, hi, _ = unit_io(u)
                        v.tensor_copy(hi, place).then_inc(unit_hi, 1)

            dve.sem_inc(y_done.sem, 1)
            steps(dve, lambda st: [slot(st, h) for h in range(H)])

        @block.gpsimd
        def _(pool):
            g = nc.gpsimd
            g.memset(minus_half[:, :], -0.5).then_inc(causal_made, 1)
            g.memset(causal[:, :, :], 0.0).then_inc(causal_made, 1)
            pool.wait_ge(causal_made, 2)
            g.affine_select(out=causal[:, :, :], in_=causal[:, :, :], compare_op=ALU.is_ge, fill=MASKED, base=0,
                            pattern=[[P, TT], [-1, S]], channel_multiplier=1).then_inc(causal_made, 1)
            pool.wait_ge(const_landed, 48)
            g.tensor_tensor(rows_sb[:, R_BO, :], rows_sb[:, R_BO, :], rows_sb[:, R_BG, :], ALU.add)\
                .then_inc(causal_made, 1)
            pool.wait_ge(causal_made, 4)

            def sub(dst, a, b, done):
                if b.dtype == F32R:
                    b = b.bitcast(F32)
                g.tensor_tensor(dst, a, b, ALU.subtract).then_inc(done, 1)

            def per_token(row):
                return rows_sb[:, row, :].unsqueeze(1).to_broadcast([P, TT, D])

            def slot(st, h):
                if h == 15 and has(st.nxt2):
                    pool.wait_ge(xt_h.sem, xt_h.after(st.nxt2))
                    sub(xt_lo[:, :, :], tf_a[:, :, :], xt_hi[:, :, :], xt_l.sem)
                if h == 3 and has(st.old, MLP):
                    pool.wait_ge(x2t_h.sem, x2t_h.after(st.old))
                    sub(x2t_lo[:, :, :], tf_b[:, :, :], x2t_hi[:, :, :], x2t_l.sem)
                if h == 4 and has(st.nxt):
                    pool.wait_ge(q_p1.sem, q_p1.after(st.nxt))
                    sub(q_f[:, :, :], q_f[:, :, :], q_part[:, 0], q_r.sem)
                if h == 5 and has(st.nxt):
                    pool.wait_ge(k_p1.sem, k_p1.after(st.nxt))
                    sub(k_f[:, :, :], k_f[:, :, :], k_part[:, 0], k_r.sem)
                    pool.wait_ge(q_p2.sem, q_p2.after(st.nxt))
                    sub(q_part[:, 2], q_f[:, :, :], q_part[:, 1], q_p3.sem)
                if h == 6 and has(st.nxt):
                    pool.wait_ge(k_p2.sem, k_p2.after(st.nxt))
                    sub(k_part[:, 2], k_f[:, :, :], k_part[:, 1], k_p3.sem)
                if h == 6 and has(st.prev, (0,)):
                    pool.wait_ge(ct_h.sem, ct_h.after(st.prev))
                    sub(ct_lo[:, :, :], tf_b[:, :, :], ct_hi[:, :, :], ct_l.sem)
                if 7 <= h <= 10 and has(st.old, MLP):
                    n = h - 7
                    pool.wait_ge(h_h.sem, h_h.after(st.old, n + 1))
                    sub(h_lo[:, 2 * n:2 * n + 2, :], h_f[:, n % 2], h_hi[:, 2 * n:2 * n + 2, :], h_l.sem)
                if h == 10 and has(st.prev, (0,)):
                    pool.wait_ge(res_landed.of(st.prev), res_landed.after(st.prev))
                    g.tensor_tensor(x_res[:, :, :], x_res[:, :, :], per_token(R_BO), ALU.add).then_inc(res_done.sem, 1)
                if h == 12 and has(st.prev):
                    pool.wait_ge(ot_h.sem, ot_h.after(st.prev))
                    sub(ot_lo[:, :, :], tf_a[:, :, :], ot_hi[:, :, :], ot_l.sem)
                if h == 12 and has(st.old, MLP):
                    pool.wait_ge(x2_hat_done.sem, x2_hat_done.after(st.old))
                    r = R_B2 + MLP.index(st.old.p)
                    g.tensor_tensor(x2[:, st.old.par], x2[:, st.old.par], per_token(r), ALU.add)\
                        .then_inc(x2b_done.sem, 1)
                if h == 10 and has(st.nxt2):
                    pool.wait_ge(ln_ve.sem, ln_ve.after(st.nxt2))
                    if st.nxt:
                        pool.wait_ge(x_hat.sem, x_hat.after(st.nxt))
                    g.tensor_tensor(rstd[:, :], ve[:, :], minus_half[:, :], ALU.pow).then_inc(ln_rstd.sem, 1)
                if h == 6 and has(st.nxt2, (2,)):
                    pool.wait_ge(ct_h.sem, ct_h.after(st.nxt2))
                    sub(ct_lo[:, :, :], tf_b[:, :, :], ct_hi[:, :, :], ct_l.sem)
                if h == 14 and has(st.prev, MLP):
                    pool.wait_ge(ln2_ve.sem, ln2_ve.after(st.prev))
                    g.tensor_tensor(rstd2[:, :], ve2[:, :], minus_half[:, :], ALU.pow).then_inc(ln2_rstd.sem, 1)
                if st.s is not None:
                    for u in UNIT_AT.get((st.s, h), ()):
                        pool.wait_ge(unit_hi, u + 1)
                        _, place, hi, lo = unit_io(u)
                        sub(lo, place, hi, unit_lo)

            steps(pool, lambda st: [slot(st, h) for h in range(H)])


def kernel(**inputs):
    import numpy as np
    import concourse.bacc as bacc
    from concourse.bass_utils import run_bass_kernel_spmd

    a = {k: np.asarray(v) for k, v in inputs.items()}
    l0 = {k[len("L0_xattn_"):]: v for k, v in a.items() if k.startswith("L0")}
    l1 = {k[len("L1_xattn_"):]: v for k, v in a.items() if k.startswith("L1")}
    none = np.zeros((D, D), np.float32)
    wa = np.stack([
        np.stack([l0[n].T for n in ("Wq", "Wk", "Wv", "Wo", "Wg")]),
        np.stack([l1["sa_" + n] for n in ("wq", "wk", "wv", "wo")] + [none]),
        np.stack([l1["ca_" + n] for n in ("wq", "wk", "wv", "wo")] + [none]),
    ])
    wm1 = np.stack([l0["W1"].T, l1["mlp_w1"]])
    wm2 = np.stack([l0["W2"].T, l1["mlp_w2"]])
    vectors = [l0["g1"], l0["be1"], l1["ln1_s"], l1["ln1_b"], l1["ln2_s"], l1["ln2_b"], l0["g2"], l0["be2"],
               l1["ln3_s"], l1["ln3_b"], l0["bq"], l0["bk"], l0["b1"], l1["mlp_b1"]]
    cols = np.concatenate([w.reshape(-1, P) for w in vectors]).T
    rows = np.stack([l0["bv"], l0["bo"], l0["bg"], l0["b2"], l1["mlp_b2"]])
    arrays = {"x": a["x"], "ctx": a["ctx_1024"], "mask": a["mask_BxSxS2_fk0"], "wa": wa, "wm1": wm1, "wm2": wm2,
              "cols": cols, "rows": rows, "ident": np.eye(P, dtype=np.float32)}
    arrays = {k: np.ascontiguousarray(v) for k, v in arrays.items()}

    nc = bacc.Bacc("TRN2", target_bir_lowering=False, num_devices=1)
    args = [nc.dram_tensor(k, v.shape, mybir.dt.from_np(v.dtype), kind="ExternalInput").ap() for k, v in arrays.items()]
    out = nc.dram_tensor("out", (B, S, D), F32, kind="ExternalOutput").ap()
    two_layers(nc, *args, out)
    r = run_bass_kernel_spmd(nc, [arrays], core_ids=[0])
    return r.results[0]["out"]
```
